# Optimizing a Trainium2 kernel written in Bass

```python
import numpy as np
import jax
import jax.numpy as jnp

def _softmax(x, axis=-1):
    return jax.nn.softmax(x, axis=axis)

def _gelu(x):
    return jax.nn.gelu(x, approximate=True)

def _silu(x):
    return jax.nn.silu(x)

def _sigmoid(x):
    return jax.nn.sigmoid(x)

def _layernorm(x, axis=-1, eps=1e-05):
    m = jnp.mean(x, axis=axis, keepdims=True)
    v = jnp.var(x, axis=axis, keepdims=True)
    return (x - m) / jnp.sqrt(v + eps)

def _scatter_add(tgt, idx, src, axis=0):
    return tgt.at[idx].add(src)

def _segment_sum(src, seg, n):
    return jax.ops.segment_sum(src, seg, n)
kernel_name = 'mk_adj_ffn_d1_adj_r2_54eb05'

def setup_inputs(seed: int=0):
    np.random.seed(seed)
    _w = jnp.asarray

    def _rec_inputs():
        import jax
        import jax.numpy as jnp
        _gk = jax.random.key(seed)
        x = -0.000929 + 1 * jax.random.normal(jax.random.fold_in(_gk, 1), (1354, 256), jnp.float32)
        _a = jax.random.bernoulli(jax.random.fold_in(_gk, 2), 0.00590842, (1354, 1354))
        _af = _a.astype(jnp.float32)
        _af = _af * jax.random.uniform(jax.random.fold_in(_gk, 3), (1354, 1354), jnp.float32, 0.05, 5.22011)
        adj = _af
        return (x, adj)
    x, adj = _rec_inputs()

    def _L0_gnn_setup():
        import jax, jax.numpy as jnp
        import numpy as np
        N = 1024
        HID = 256
        H = 8
        key = jax.random.key(seed)
        ks = jax.random.split(key, 8)
        x = jax.random.normal(ks[0], (N, HID), dtype=jnp.float32)
        sp = jax.random.normal(ks[1], (N, N), dtype=jnp.float32)
        zero_mask = jax.random.uniform(ks[2], (N, N)) < 0.2
        spatial_encoding = jnp.where(zero_mask, 0.0, sp)
        edge_encoding = jax.random.normal(ks[3], (N, N), dtype=jnp.float32)
        s = 1.0 / np.sqrt(HID)
        Wq = jax.random.normal(ks[4], (HID, HID * H), dtype=jnp.float32) * s
        Wk = jax.random.normal(ks[5], (HID, HID * H), dtype=jnp.float32) * s
        Wv = jax.random.normal(ks[6], (HID, HID * H), dtype=jnp.float32) * s
        Wout = jax.random.normal(ks[7], (HID * H, HID), dtype=jnp.float32) * (1.0 / np.sqrt(HID * H))
        return {'x': x, 'spatial_encoding': spatial_encoding, 'edge_encoding': edge_encoding, 'Wq': Wq, 'Wk': Wk, 'Wv': Wv, 'Wout': Wout}
    _L0_gnn_all = _L0_gnn_setup()
    _L0_gnn_in = {k: v for k, v in _L0_gnn_all.items() if k in ('Wq', 'Wk', 'Wv', 'Wout')}
    del _L0_gnn_all

    def _L0_ffn_setup():
        import jax, jax.numpy as jnp
        import numpy as np
        D_MODEL = 256
        D_FF = 1024
        NUM_EXPERTS = 8
        TOP_K = 2
        key = jax.random.key(seed)
        ks = jax.random.split(key, 7)
        B, S = (4, 1024)
        x = jax.random.normal(ks[0], (B, S, D_MODEL), dtype=jnp.float32)
        Wg = jax.random.normal(ks[1], (D_MODEL, NUM_EXPERTS), dtype=jnp.float32) * (1.0 / np.sqrt(D_MODEL))
        bg = jnp.zeros((NUM_EXPERTS,), dtype=jnp.float32)
        W1 = jax.random.normal(ks[2], (NUM_EXPERTS, D_MODEL, D_FF), dtype=jnp.float32) * (1.0 / np.sqrt(D_MODEL))
        b1 = jnp.zeros((NUM_EXPERTS, D_FF), dtype=jnp.float32)
        W2 = jax.random.normal(ks[3], (NUM_EXPERTS, D_FF, D_MODEL), dtype=jnp.float32) * (1.0 / np.sqrt(D_FF))
        b2 = jnp.zeros((NUM_EXPERTS, D_MODEL), dtype=jnp.float32)
        return {'x': x, 'Wg': Wg, 'bg': bg, 'W1': W1, 'b1': b1, 'W2': W2, 'b2': b2}
    _L0_ffn_all = _L0_ffn_setup()
    _L0_ffn_in = {k: v for k, v in _L0_ffn_all.items() if k in ('Wg', 'bg', 'W1', 'b1', 'W2', 'b2')}
    del _L0_ffn_all
    return {'x': x, 'adj': adj, 'L0_gnn_Wq': _L0_gnn_in['Wq'], 'L0_gnn_Wk': _L0_gnn_in['Wk'], 'L0_gnn_Wv': _L0_gnn_in['Wv'], 'L0_gnn_Wout': _L0_gnn_in['Wout'], 'L0_ffn_Wg': _L0_ffn_in['Wg'], 'L0_ffn_bg': _L0_ffn_in['bg'], 'L0_ffn_W1': _L0_ffn_in['W1'], 'L0_ffn_b1': _L0_ffn_in['b1'], 'L0_ffn_W2': _L0_ffn_in['W2'], 'L0_ffn_b2': _L0_ffn_in['b2']}

def reference(x, adj, L0_gnn_Wq, L0_gnn_Wk, L0_gnn_Wv, L0_gnn_Wout, L0_ffn_Wg, L0_ffn_bg, L0_ffn_W1, L0_ffn_b1, L0_ffn_W2, L0_ffn_b2):
    import jax
    import jax.numpy as jnp

    def _L0_gnn_ref(x, spatial_encoding, edge_encoding, Wq, Wk, Wv, Wout):
        import jax, jax.numpy as jnp
        import numpy as np
        N = 1024
        HID = 256
        H = 8
        n, d = x.shape
        h = Wq.shape[1] // d
        scale = d ** (-0.5)
        q = (x @ Wq).reshape(h, n, d)
        k = (x @ Wk).reshape(h, n, d)
        v = (x @ Wv).reshape(h, n, d)
        a = jnp.einsum('hnd,hmd->hnm', q, k) * scale
        a = a + spatial_encoding + edge_encoding
        mask = spatial_encoding == 0.0
        a = jnp.where(mask, -1000000.0, a)
        a = jax.nn.softmax(a, axis=-1)
        a = jnp.where(mask, 0.0, a)
        out = jnp.einsum('hnm,hmd->hnd', a, v)
        out = out.transpose(1, 0, 2).reshape(n, h * d)
        return out @ Wout

    def _L0_ffn_ref(x, Wg, bg, W1, b1, W2, b2):
        import jax, jax.numpy as jnp
        import numpy as np
        D_MODEL = 256
        D_FF = 1024
        NUM_EXPERTS = 8
        TOP_K = 2
        B, S, D = x.shape
        x_flat = x.reshape(-1, D)
        gate_logits = x_flat @ Wg + bg
        gate_logits = gate_logits - jnp.max(gate_logits, axis=-1, keepdims=True)
        gate_top_k, gate_idx = jax.lax.top_k(gate_logits, TOP_K)
        gate_scores = jax.nn.softmax(gate_top_k, axis=-1)
        h = jax.nn.gelu(jnp.einsum('td,edf->etf', x_flat, W1) + b1[:, None, :], approximate=False)
        expert_out = jnp.einsum('etf,efd->etd', h, W2) + b2[:, None, :]
        expert_out = jnp.transpose(expert_out, (1, 0, 2))
        topk_out = jnp.take_along_axis(expert_out, gate_idx[:, :, None], axis=1)
        moe_out = jnp.sum(topk_out * gate_scores[:, :, None], axis=1)
        return moe_out.reshape(B, S, D) + x
    x = x + _L0_gnn_ref(_layernorm(x, axis=-1), adj, adj, L0_gnn_Wq, L0_gnn_Wk, L0_gnn_Wv, L0_gnn_Wout)
    x = x + _L0_ffn_ref(_layernorm(x, axis=-1)[None], L0_ffn_Wg, L0_ffn_bg, L0_ffn_W1, L0_ffn_b1, L0_ffn_W2, L0_ffn_b2)[0]
    return x

_drawn_inputs = setup_inputs


def setup_inputs(seed=0):
    import zlib

    import numpy as np

    out = dict(_drawn_inputs(seed))
    spreads = {'L0_ffn_bg': (0.0, 0.1), 'L0_ffn_b1': (0.0, 0.354), 'L0_ffn_b2': (0.0, 0.1)}
    factors = {}
    for name, (base, spread) in spreads.items():
        noise = np.random.default_rng([zlib.crc32(name.encode()), seed]).standard_normal(out[name].shape)
        drawn = base * np.exp(spread * noise) if base else spread * noise
        out[name] = jnp.asarray(drawn.astype(out[name].dtype))
    for name, factor in factors.items():
        out[name] = (out[name] * factor).astype(out[name].dtype)
    return out
```

```python
from contextlib import ExitStack

import concourse.bass as bass
from concourse import mybir

ALU = mybir.AluOpType
ACT = mybir.ActivationFunctionType
AX = mybir.AxisListType
F32 = mybir.dt.float32
F16 = mybir.dt.float16
I32 = mybir.dt.int32
U32 = mybir.dt.uint32

P = 128
N = 1354
D = 256
H = 8
E = 8
FF = 1024
DT = D // P
FT = FF // P
T = (N + P - 1) // P
TAIL = N - (T - 1) * P
TP = T // 2
NP = T * P
BLOCKS = (2 * N + E * (P - 1)) // P
WIN = N // 8 + 2
PAD = 16
QW = PAD + NP
CH = [(0, 512), (512, 512), (1024, N - 1024)]
PG = [(0, 4), (4, 4), (8, T - 8)]
GROUPS = 15
EPS = 1e-5

S_X = 2.0 ** 8
S_W = 2.0 ** 9
S_Q = 2.0 ** 5
S_V = 2.0 ** 8
S_P = 2.0 ** 12
S_H = 2.0 ** 6
S_LOGIT = S_Q * S_Q * 16.0
HALF = 0.5
S_ACC = S_P * S_V
MASKED = -1.0e6


class Map:

    def __init__(self, arena):
        self.arena, self.at = arena, 0

    def take(self, cols, dt):
        size = 4 if dt in (F32, I32, U32) else 2
        view = self.arena[:, self.at // 2:(self.at + cols * size) // 2]
        self.at += cols * size
        return view if dt == F16 else view.bitcast(dt)


def build(nc, x, adj, Wq, Wk, Wv, Wout, Wg, bg, W1, b1, W2, b2, out, w_split, xs, ys):
    with ExitStack() as ctx:
        def sb(name, shape, dt):
            return ctx.enter_context(nc.sbuf_tensor(name, shape, dt))

        def sem(name):
            return ctx.enter_context(nc.semaphore(name))

        ARENA = 198528 // 2
        arena = sb("arena", [P, ARENA], F16)
        acc = sb("acc", [P, T, D], F32)
        ident = sb("ident", [P, P], F32)
        ident16 = sb("ident16", [P, P], F16)
        wscale = sb("wscale", [P, 1], F32)
        zero = sb("zero", [P, 1], F32)
        b1T = sb("b1T", [P, E * FT], F32)
        sums = sb("sums", [P, T], F32)
        rowmax = sb("rowmax", [P, T], F32)
        chunkmax = sb("chunkmax", [P, 3], F32)
        pool_credit = sb("pool_credit", [P, 1], F32)
        dve_credit = sb("dve_credit", [P, 2], F32)
        shift = sb("shift", [P, 1], F32)
        recip = sb("recip", [P, 1], F32)
        norm = sb("norm", [P, 1], F32)
        stats = sb("stats", [P, T, 6], F32)
        meanvar = sb("meanvar", [P, T, 2], F32)
        std = sb("std", [P, T], F32)
        rstd = sb("rstd", [P, T], F32)

        m = Map(arena)
        wqkv = [m.take(2 * DT * H * D, F16).rearrange("p (s f n) -> p s f n", s=2, f=DT) for _ in range(3)]
        wk_s, wq_s, wv_s = wqkv
        xnT = m.take(2 * DT * NP, F16).rearrange("p (s f n) -> p s f n", s=2, f=DT)
        vT = m.take(2 * DT * QW, F16).rearrange("p (s f n) -> p s f n", s=2, f=DT)
        kT = m.take(2 * DT * QW, F16).rearrange("p (s f n) -> p s f n", s=2, f=DT)
        at_q = m.at
        qT = m.take(2 * DT * QW, F16).rearrange("p (s f n) -> p s f n", s=2, f=DT)
        m2 = Map(arena)
        m2.at = at_q
        xn = m2.take(T * D, F32).rearrange("p (t d) -> p t d", d=D)
        vo = m.take(2 * T * D, F16).rearrange("p (s t d) -> p s t d", s=2, d=D)
        wo_s = m.take(2 * DT * D, F16).rearrange("p (s f n) -> p s f n", s=2, f=DT)
        wo_in = m.take(DT * D, F32).rearrange("p (f n) -> p f n", f=DT)
        bias = m.take(T * N, F32).rearrange("p (t n) -> p t n", n=N)
        logits = m.take(N, F32)
        prob = m.take(NP, F32)
        probT = m.take(2 * NP, F16).rearrange("p (s n) -> p s n", s=2)
        stage = m.take(3 * 1024, F32).rearrange("p (s n) -> p s n", s=3)
        assert m.at <= 2 * ARENA, m.at
        split_out = stage[:, 2, :].bitcast(F16).rearrange("p (s n) -> p s n", s=2)
        b1rows = logits[0:E * FT, 0:P]
        masked = stage[:, 0:2, :].rearrange("p s n -> p (s n)")[:, 0:N]
        zeros = stage[:, 2, 0:D].bitcast(F16)

        f = Map(arena)
        we = f.take(E * 8192, F16).rearrange("p (e n) -> p e n", e=E)
        w1_s = [we[:, :, 2048 * s:2048 * (s + 1)].rearrange("p e (f n) -> p e f n", f=DT) for s in range(2)]
        w2_s = [we[:, :, 4096 + 2048 * s:4096 + 2048 * (s + 1)].rearrange("p e (f n) -> p e f n", f=FT)
                for s in range(2)]
        f_xb = f.take(2 * BLOCKS * D, F16)
        xb = f_xb.bitcast(F32).rearrange("p (j d) -> p j d", d=D)
        ynsp = we[:, E - 1, 0:T * 2 * D].rearrange("p (t s d) -> p t s d", s=2, d=D)
        yn = f.take(T * D, F32).rearrange("p (t d) -> p t d", d=D)
        b2bc = f.take(E * D, F32).rearrange("p (e d) -> p e d", d=D)
        hid = f.take(FF, F32)
        hT = f.take(2 * FF, F16).rearrange("p (s f n) -> p s f n", s=2, f=FT)
        xT = f.take(2 * D, F16).rearrange("p (s f n) -> p s f n", s=2, f=DT)
        wg_sb = f.take(DT * E, F32).rearrange("p (f e) -> p f e", f=DT)
        bgbc = f.take(E, F32)
        glog = f.take(T * E, F32).rearrange("p (t e) -> p t e", e=E)
        top8 = f.take(T * E, F32).rearrange("p (t e) -> p t e", e=E)
        idx8 = f.take(T * E, U32).rearrange("p (t e) -> p t e", e=E)
        idxf = f.take(T * E, F32).rearrange("p (t e) -> p t e", e=E)
        one1 = f.take(T * E, F32).rearrange("p (t e) -> p t e", e=E)
        one2 = f.take(T * E, F32).rearrange("p (t e) -> p t e", e=E)
        chosen = f.take((T + 1) * E, F32).rearrange("p (t e) -> p t e", e=E)
        rowok = f.take((T + 1) * E, F32).rearrange("p (t e) -> p t e", e=E)
        slot_e = f.take(T * E, F32).rearrange("p (t e) -> p t e", e=E)
        pick = f.take(T * E, F32).rearrange("p (t e) -> p t e", e=E)
        slotf = f.take(2 * T, F32).rearrange("p (k t) -> p k t", k=2)
        slot = f.take(2 * T, U32).rearrange("p (k t) -> p k t", k=2)
        gate = f.take(2 * T, F32).rearrange("p (k t) -> p k t", k=2)
        gap = f.take(T, F32)
        expgap = f.take(T, F32)
        den = f.take(T, F32)
        countsi = f.take(E, I32)
        padi = f.take(E, I32)
        padf = f.take(E, F32)
        ends = f.take(E, F32)
        base = f.take(E, F32)
        onesr = f.take(E, F32)
        iota_i = f.take(E, I32)
        iota_f = f.take(E, F32)
        jb_i = f.take(BLOCKS, I32)
        jb_f = f.take(BLOCKS, F32)
        jcmp = f.take(BLOCKS * E, F32).rearrange("p (j e) -> p j e", e=E)
        jexp = f.take(BLOCKS, F32)
        block_expert = f.take(BLOCKS, I32)
        tri = f.take(P, F32)
        ones = f.take(P, F32)
        assert f.at <= 2 * ARENA, f.at
        g = Map(arena)
        back = g.take(2 * T * D, F32).rearrange("p (k t d) -> p k t d", k=2, d=D)
        xb16 = f_xb.rearrange("p (j n) -> p j n", n=2 * D)
        ynT = xb.rearrange("p j d -> p (j d)")[:, 0:DT * NP].rearrange("p (f n) -> p f n", f=DT)

        ps = ctx.enter_context(nc.psum_tensor("ps", [P, 8, 512], F32))
        flat = ps[:, :, :].rearrange("p b n -> p (b n)")
        S_BANK = (6, 7, 5)
        T_BANK, O_BANK = 1, 0
        xt_bank = ps[:, 0, 0:D].bitcast(F16)
        X_BANK, H_BANK, Y_BANK = 0, 1, 3

        names = """consts_ready x_tail_zero x_loaded b1_loaded stats_done meanvar_done var_done std_done rstd_done
            xn_ready xT_done xT_hi xT_lo b1_done b1_ready w_loaded0 w_loaded1 w_loaded2 w_hi w_lo
            masks_made masks_ready pads_ready prob_pad zeros_ready xs_zeroed
            wo_free wo_loaded wo_hi wo_ready proj_done proj_hi proj_lo
            qk_done logits_done chunkmax_done rowmax_ready shift_ready exp_done t_done p_hi p_lo av_done recip_ready norm_ready acc_done
            stage_free piece_loaded0 piece_loaded1 piece_hi piece_scaled piece_split piece_stored
            x1_ready stats2_done meanvar2_done var2_done std2_done rstd2_done yn_ready base_ready ynT_done ynT_ready ynsp_hi ynsp_lo
            gate_in gate_done glog_ready top8_ready idx_ready idxf_ready gap_ready expgap_ready den_ready gate1_ready
            gate_ready onehot_ready chosen_sum chosen_ready rank_done countsi_ready padi_ready padf_ready ends_ready
            base_e_ready slot_e_ready pick_ready slotf_ready slot_ready jcmp_ready jexp_ready jmin_ready block_expert_ready route_consts
            b2_loaded scattered experts_ready ex_T ex_x ex_h gelu_done ex_h_hi ex_h_lo ex_o ys_ready
            ys_stored mix1 out_ready out_stored""".split()
        s = {n: sem(n) for n in names}
        expert_loaded = [sem(f"expert_loaded{e}") for e in range(E)]
        XB = [(0, 1), (1, BLOCKS)]
        xb_in = [sem(f"xb_in{k}") for k in range(len(XB))]
        gathered = [sem(f"gathered{t}") for t in range(T)]

        def head_start(h):
            return 169 * h + h // 4, PAD - (2 * h - 8 * (h // 4))

        assert N // 8 == 169 and N % 8 == 2
        PAIR = (4, 6, 2, 0) * 3 + (2, 0, 4)

        def pair(k):
            b = PAIR[k]
            return ps[:, b:b + 2, :].rearrange("p b (j n) -> p (b j) n", j=2)

        def group_io(k, part, c0):
            if k >= 12:
                a, n = PG[k - 12]
                return vo[:, part, a:a + n, :], pair(k)[:, 0:n, :], S_V / (S_Q * S_W)
            buf, q = (kT, qT, vT)[k // 4], k % 4
            rows = buf[:, part, q // 2, bass.ds(c0, 8 * WIN)].rearrange("p (t b) -> p b t", b=8)
            return rows[:, 4 * (q % 2):4 * (q % 2) + 4, :], pair(k)[:, :, 0:WIN], S_Q / (S_X * S_W)

        def col(buf, t):
            return buf[:, bass.ds(t, 1)]

        def sl(buf, t):
            return buf[:, bass.ds(t, 1), :].rearrange("p t n -> p (t n)")

        W1r = W1.rearrange("e k n -> (e k) n")
        W2r = W2.rearrange("e k n -> (e k) n")
        ADJ = [(0, 1), (1, 5), (5, T - 1), (T - 1, T)]
        adj_in = [sem(f"adj_in{k}") for k in range(len(ADJ))]

        block = ctx.enter_context(nc.Block())

        @block.sync
        def _(sp):
            sp.wait_ge(s["x_tail_zero"], 1)
            sp.dma_start(acc[:, 0:T - 1, :], x[0:(T - 1) * P, :].rearrange("(t p) d -> p t d", p=P)).then_inc(s["x_loaded"], 16)
            sp.dma_start(acc[0:TAIL, T - 1, :], x[(T - 1) * P:N, :]).then_inc(s["x_loaded"], 16)
            sp.dma_start(b1rows, b1.rearrange("e (f p) -> (e f) p", p=P)).then_inc(s["b1_loaded"], 16)
            c = 0
            for w in (Wk, Wq, Wv):
                for ft in range(DT):
                    for half in range(2):
                        if c >= 3:
                            sp.wait_ge(s["w_lo"], c - 2)
                        sp.dma_start(stage[:, c % 3, :], w[ft * P:(ft + 1) * P, half * 1024:(half + 1) * 1024]
                                     ).then_inc(s[f"w_loaded{c % 3}"], 16)
                        c += 1
            sp.wait_ge(s["zeros_ready"], 1)
            sp.dma_start(xs.rearrange("(j p) d -> p j d", p=P), zeros.unsqueeze(1).to_broadcast([P, BLOCKS, 2 * D])
                         ).then_inc(s["xs_zeroed"], 16)
            with sp.Fori(0, H) as h:
                sp.wait_ge(s["wo_free"], h + 1)
                sp.dma_start(wo_in, Wout[bass.ds(h * D, D), :].rearrange("(f p) n -> p f n", p=P)).then_inc(s["wo_loaded"], 16)
                for q in range(4):
                    sp.wait_ge(s["stage_free"], h * 4 + q + 1)
                    if q < 2:
                        src = W1r[bass.ds(h * D + q * P, P), :]
                        dst = stage[:, q % 2, :]
                    else:
                        src = W2r[bass.ds(h * FF + (q - 2) * 512, 512), :].rearrange("(f p) n -> p f n", p=P)
                        dst = stage[:, q % 2, :].rearrange("p (f n) -> p f n", n=D)
                    sp.dma_start(dst, src).then_inc(s[f"piece_loaded{q % 2}"], 16)
            sp.wait_ge(s["piece_stored"], 16 * 4 * E)
            sp.wait_ge(s["proj_done"], GROUPS * H)
            for e in range(E):
                if e == 4:
                    sp.wait_ge(s["acc_done"], T * H + 1)
                    sp.dma_start(wg_sb, Wg.rearrange("(f p) e -> p f e", p=P)).then_inc(s["gate_in"], 16)
                    sp.dma_start(bgbc, bg.partition_broadcast(P)).then_inc(s["gate_in"], 16)
                    sp.dma_start(b2bc, b2.partition_broadcast(P)).then_inc(s["b2_loaded"], 16)
                if e == E - 1:
                    sp.wait_ge(s["scattered"], 16 * 2 * T)
                sp.dma_start(we[:, e, :].rearrange("p (k n) -> p k n", k=4), w_split[e * P:(e + 1) * P, :, :]).then_inc(expert_loaded[e], 16)
            for e in range(E):
                sp.wait_ge(expert_loaded[e], 16)
                sp.sem_inc(s["experts_ready"], 1)
            with sp.Fori(0, BLOCKS) as j:
                sp.wait_ge(s["ys_ready"], j + 1)
                sp.dma_start(ys[bass.ds(j * P, P), :], xb[:, bass.ds(j, 1), :].rearrange("p j d -> p (j d)")).then_inc(s["ys_stored"], 16)
            with sp.Fori(0, T - 1) as t:
                sp.wait_ge(s["out_ready"], t + 1)
                sp.dma_start(out[bass.ds(t * P, P), :], acc[:, bass.ds(t, 1), :].rearrange("p t d -> p (t d)")).then_inc(s["out_stored"], 16)
            sp.wait_ge(s["out_ready"], T)
            sp.dma_start(out[(T - 1) * P:N, :], acc[0:TAIL, T - 1, :]).then_inc(s["out_stored"], 16)
            sp.wait_ge(s["out_stored"], 16 * T)

        @block.gpsimd
        def _(pool):
            gp = nc.gpsimd
            gp.memset(ident[:], 0.0).then_inc(s["consts_ready"], 1)
            pool.wait_ge(s["consts_ready"], 1)
            gp.affine_select(out=ident[:], in_=ident[:], compare_op=ALU.not_equal, fill=1.0, base=0,
                             pattern=[[-1, P]], channel_multiplier=1).then_inc(s["consts_ready"], 1)
            pool.wait_ge(s["consts_ready"], 2)
            gp.tensor_scalar(ident16[:], ident[:], 1.0, None, ALU.mult).then_inc(s["consts_ready"], 1)
            gp.memset(wscale[:], S_W).then_inc(s["consts_ready"], 1)
            gp.memset(zero[:], 0.0).then_inc(s["consts_ready"], 1)
            gp.memset(prob[:, N:NP], 0.0).then_inc(s["prob_pad"], 1)
            gp.memset(bias[:, T - 1, :], 0.0).then_inc(s["masks_made"], 1)
            for k, (a, b) in enumerate(ADJ):
                if k < len(ADJ) - 1:
                    gp.dma_start(bias[:, a:b, :], adj[a * P:b * P, :].rearrange("(t p) n -> p t n", p=P)).then_inc(adj_in[k], 16)
                else:
                    pool.wait_ge(s["masks_made"], 1)
                    gp.dma_start(bias[0:TAIL, a, :], adj[a * P:N, :]).then_inc(adj_in[k], 16)
            pool.wait_ge(s["w_lo"], 12)
            gp.memset(zeros, 0.0).then_inc(s["zeros_ready"], 1)
            for k, (a, b) in enumerate(ADJ):
                pool.wait_ge(adj_in[k], 16)
                for t in range(a, b):
                    row = bias[:, t, :]
                    gp.tensor_scalar(masked, row, 0.0, HALF * MASKED, ALU.is_equal, ALU.mult).then_inc(s["masks_made"], 1)
                    pool.wait_ge(s["masks_made"], t + 2)
                    gp.tensor_tensor(row, row, masked, ALU.add).then_inc(s["masks_ready"], 1)
                    pool.wait_ge(s["masks_ready"], t + 1)
            pool.wait_ge(s["consts_ready"], 5)
            pool.wait_ge(s["xs_zeroed"], 16)
            gp.memset(pool_credit[:], 0.0).then_inc(s["stage_free"], 2)
            with pool.Fori(0, E) as e:
                for q in range(4):
                    n = e * 4 + q
                    src = stage[:, q % 2, :]
                    pool.wait_ge(s[f"piece_loaded{q % 2}"], 32 * e + 16 * (q // 2) + 16)
                    gp.tensor_tensor(src, src, wscale[:].to_broadcast([P, 1024]), ALU.mult).then_inc(s["piece_scaled"], 1)
                    pool.wait_ge(s["piece_scaled"], n + 1)
                    gp.tensor_tensor(split_out[:, 0, :], src, zero[:].to_broadcast([P, 1024]), ALU.add).then_inc(s["piece_hi"], 1)
                    pool.wait_ge(s["piece_hi"], n + 1)
                    gp.tensor_tensor(split_out[:, 1, :], src, split_out[:, 0, :], ALU.subtract).then_inc(s["stage_free"], 1)
                    pool.wait_ge(s["stage_free"], n + 3)
                    a, c = 2 * (q // 2), (q % 2) * 1024
                    dst = w_split[bass.ds(e * P, P), a:a + 2, c:c + 1024]
                    gp.dma_start(dst, split_out).then_inc(s["piece_stored"], 16)
                    pool.wait_ge(s["piece_stored"], 16 * n + 16)
            pool.wait_ge(s["acc_done"], T * H + 1)
            pool.wait_ge(s["piece_stored"], 16 * 4 * E)
            gp.memset(chosen, 0.0).then_inc(s["route_consts"], 1)
            gp.memset(rowok, 1.0).then_inc(s["route_consts"], 1)
            gp.memset(tri, 1.0).then_inc(s["route_consts"], 1)
            gp.memset(ones, 1.0).then_inc(s["route_consts"], 1)
            gp.memset(onesr, 1.0).then_inc(s["route_consts"], 1)
            gp.iota(iota_i, pattern=[[1, E]], base=0, channel_multiplier=0).then_inc(s["route_consts"], 1)
            gp.iota(jb_i, pattern=[[P, BLOCKS]], base=0, channel_multiplier=0).then_inc(s["route_consts"], 1)
            pool.wait_ge(s["route_consts"], 7)
            gp.affine_select(out=rowok, in_=rowok, compare_op=ALU.is_ge, fill=0.0, base=N - 1,
                             pattern=[[-P, T + 1], [0, E]], channel_multiplier=-1).then_inc(s["route_consts"], 1)
            gp.affine_select(out=tri, in_=tri, compare_op=ALU.is_ge, fill=0.0, base=-1,
                             pattern=[[1, P]], channel_multiplier=-1).then_inc(s["route_consts"], 1)
            pool.wait_ge(s["slot_ready"], 1)
            pool.wait_ge(s["ynsp_lo"], 1)
            for k in range(2):
                for t in range(T):
                    rows = P if t < T - 1 else TAIL
                    gp.indirect_dma_start(xs[:, :], bass.IndirectOffsetOnAxis(ap=slot[0:rows, k, t:t + 1], axis=0),
                                          ynsp[0:rows, t, :, :].rearrange("p s d -> p (s d)"), None).then_inc(s["scattered"], 16)
            pool.wait_ge(s["scattered"], 16 * 2 * T)
            pool.wait_ge(s["ynT_done"], TP + 1)
            pool.wait_ge(s["gate_done"], 1)
            for k, (a, b) in enumerate(XB):
                gp.dma_start(xb16[:, a:b, :], xs[a * P:b * P, :].rearrange("(j p) d -> p j d", p=P)).then_inc(xb_in[k], 16)
            pool.wait_ge(s["ys_stored"], 16 * BLOCKS)
            pool.wait_ge(s["ex_o"], BLOCKS)
            for t in range(T):
                for k in range(2):
                    rows = P if t < T - 1 else TAIL
                    gp.indirect_dma_start(back[0:rows, k, t, :], None, ys[:, :],
                                          bass.IndirectOffsetOnAxis(ap=slot[0:rows, k, t:t + 1], axis=0)).then_inc(gathered[t], 16)

        @block.scalar
        def _(act):
            A = nc.scalar

            def copy(dst, src, scale):
                return A.activation(dst, src, ACT.Copy, scale=scale)

            act.wait_ge(s["var_done"], 1)
            A.activation(std[:], std[:], ACT.Sqrt).then_inc(s["std_done"], 1)
            for k in range(TP + 1):
                w = 2 * P if k < TP else P
                act.wait_ge(s["xT_done"], k + 1)
                copy(xnT[:, 0, :, 2 * P * k:2 * P * k + w], ps[:, k, 0:2 * w].rearrange("p (f n) -> p f n", f=DT), S_X
                     ).then_inc(s["xT_hi"], 1)
            for c in range(12):
                act.wait_ge(s[f"w_loaded{c % 3}"], 16 * (c // 3 + 1))
                copy(wqkv[c // 4][:, 0, (c // 2) % 2, (c % 2) * 1024:(c % 2 + 1) * 1024], stage[:, c % 3, :], S_W).then_inc(s["w_hi"], 1)

            def probs(h, t):
                i = h * T + t
                act.wait_ge(s["shift_ready"], i + 1)
                A.activation(prob[:, 0:N], logits, ACT.Exp, bias=shift[:], scale=1.0 / HALF,
                             accum_out=col(sums, t)).then_inc(s["exp_done"], 1)

            def probs_hi(i):
                for g_, (c0, k) in enumerate(PG):
                    act.wait_ge(s["t_done"], 3 * i + g_ + 1)
                    copy(probT[:, 0, c0 * P:(c0 + k) * P], ps[:, T_BANK + g_, 0:k * P], S_P).then_inc(s["p_hi"], 1)

            with act.Fori(0, H) as h:
                _, c0 = head_start(h)
                act.wait_ge(s["wo_loaded"], 16 * h + 16)
                copy(wo_s[:, 0, :, :], wo_in, S_W).then_inc(s["wo_hi"], 1)
                for k in range(GROUPS):
                    if k == 12:
                        probs(h, 0)
                    act.wait_ge(s["proj_done"], GROUPS * h + k + 1)
                    dst, src, scale = group_io(k, 0, c0)
                    copy(dst, src, scale).then_inc(s["proj_hi"], 1)
                with act.Fori(0, T - 1) as t:
                    i = h * T + t
                    probs_hi(i)
                    probs(h, t + 1)
                probs_hi(h * T + T - 1)

            act.wait_ge(s["var2_done"], 1)
            A.activation(std[:], std[:], ACT.Sqrt).then_inc(s["std2_done"], 1)
            for k in range(TP + 1):
                w = 2 * P if k < TP else P
                act.wait_ge(s["ynT_done"], k + 1)
                A.activation(ynT[:, :, 2 * P * k:2 * P * k + w], ps[:, k, 0:2 * w].rearrange("p (f n) -> p f n", f=DT),
                             ACT.Copy).then_inc(s["ynT_ready"], 1)
            act.wait_ge(s["gap_ready"], 1)
            A.activation(expgap, gap, ACT.Exp).then_inc(s["expgap_ready"], 1)
            act.wait_ge(s["block_expert_ready"], 1)
            with act.Fori(0, BLOCKS) as j:
                e = A.value_load(block_expert[0:1, bass.ds(j, 1)], min_val=0, max_val=E - 1)
                for ft in range(FT):
                    if ft % 4 == 0:
                        act.wait_ge(s["ex_h"], 2 * j + ft // 4 + 1)
                        act.wait_ge(s["ex_h_lo"], 2 * j + ft // 4 + 1)
                    last = A.activation(hid[:, ft * P:(ft + 1) * P], flat[:, 512 * H_BANK + ft * P:512 * H_BANK + (ft + 1) * P],
                                        ACT.Gelu, bias=b1T[:, bass.ds(e * FT + ft, 1)], scale=1.0 / (S_X * S_W))
                    if ft % 4 == 3:
                        last.then_inc(s["gelu_done"], 1)

        @block.vector
        def _(dve):
            V = nc.vector

            def layernorm(tag, dst, eps_sem):
                with dve.Fori(0, T) as t:
                    V.bn_stats(sl(stats, t), sl(acc, t)).then_inc(s["stats%s_done" % tag], 1)
                dve.wait_ge(s["stats%s_done" % tag], T)
                for t in range(T):
                    V.bn_aggr(meanvar[:, t, :], stats[:, t, :]).then_inc(s["meanvar%s_done" % tag], 1)
                dve.wait_ge(s["meanvar%s_done" % tag], T)
                V.tensor_scalar(std[:], meanvar[:, :, 1], EPS, None, ALU.add).then_inc(s["var%s_done" % tag], 1)
                dve.wait_ge(s["std%s_done" % tag], 1)
                V.reciprocal(rstd[:], std[:]).then_inc(s["rstd%s_done" % tag], 1)
                dve.wait_ge(s["rstd%s_done" % tag], 1)
                with dve.Fori(0, T) as t:
                    mean = meanvar[:, bass.ds(t, 1), 0:1].rearrange("p t k -> p (t k)")
                    V.tensor_scalar(sl(dst, t), sl(acc, t), mean, col(rstd, t), ALU.subtract, ALU.mult).then_inc(eps_sem, 1)

            V.memset(acc[:, T - 1, :], 0.0).then_inc(s["x_tail_zero"], 1)
            dve.wait_ge(s["x_loaded"], 32)
            layernorm("", xn, s["xn_ready"])
            dve.wait_ge(s["xn_ready"], T)
            V.tensor_scalar(acc[:, :, :], acc[:, :, :], S_ACC, None, ALU.mult).then_inc(s["acc_done"], 1)
            for k in range(TP + 1):
                w = 2 * P if k < TP else P
                dve.wait_ge(s["xT_hi"], k + 1)
                V.scalar_tensor_tensor(xnT[:, 1, :, 2 * P * k:2 * P * k + w], ps[:, k, 0:2 * w].rearrange("p (f n) -> p f n", f=DT),
                                       S_X, xnT[:, 0, :, 2 * P * k:2 * P * k + w], ALU.mult, ALU.subtract).then_inc(s["xT_lo"], 1)
            dve.wait_ge(s["b1_done"], 1)
            V.tensor_copy(b1T[:], ps[:, 6, 0:E * FT]).then_inc(s["b1_ready"], 1)
            V.memset(qT[:, :, :, PAD + N - 8:QW], 0.0).then_inc(s["pads_ready"], 1)
            V.memset(vT[:, :, :, PAD + N - 8:QW], 0.0).then_inc(s["pads_ready"], 1)
            for c in range(12):
                w = wqkv[c // 4][:, :, (c // 2) % 2, (c % 2) * 1024:(c % 2 + 1) * 1024]
                dve.wait_ge(s["w_hi"], c + 1)
                last = V.scalar_tensor_tensor(w[:, 1, :], stage[:, c % 3, :], S_W, w[:, 0, :], ALU.mult, ALU.subtract)
                last.then_inc(s["w_lo"], 1)
            V.memset(dve_credit[:, 0:1], 0.0).then_inc(s["wo_free"], 1)

            def row_logits(h, t, c):
                i = h * T + t
                c0, w = CH[c]
                dve.wait_ge(s["qk_done"], 3 * i + c + 1)
                if c == 0:
                    dve.wait_ge(s["masks_ready"], t + 1)
                V.scalar_tensor_tensor(logits[:, c0:c0 + w], ps[:, S_BANK[c], 0:w], HALF / S_LOGIT,
                                       bias[:, bass.ds(t, 1), c0:c0 + w].rearrange("p t n -> p (t n)"),
                                       ALU.mult, ALU.add).then_inc(s["logits_done"], 1)

            def row_max(h, t, c):
                c0, w = CH[c]
                dve.wait_ge(s["logits_done"], 3 * (h * T + t) + c + 1)
                V.tensor_reduce(chunkmax[:, c:c + 1], logits[:, c0:c0 + w], AX.X, ALU.max).then_inc(s["chunkmax_done"], 1)

            def row_shift(h, t):
                i = h * T + t
                dve.wait_ge(s["chunkmax_done"], 3 * i + 3)
                V.tensor_reduce(col(rowmax, t), chunkmax[:, 0:3], AX.X, ALU.max).then_inc(s["rowmax_ready"], 1)
                dve.wait_ge(s["rowmax_ready"], i + 1)
                V.tensor_scalar(shift[:], col(rowmax, t), -1.0 / HALF, None, ALU.mult).then_inc(s["shift_ready"], 1)

            def probs_lo(i, g_):
                c0, k = PG[g_]
                dve.wait_ge(s["p_hi"], 3 * i + g_ + 1)
                V.scalar_tensor_tensor(probT[:, 1, c0 * P:(c0 + k) * P], ps[:, T_BANK + g_, 0:k * P], S_P,
                                       probT[:, 0, c0 * P:(c0 + k) * P], ALU.mult, ALU.subtract).then_inc(s["p_lo"], 1)

            def gather_rows(h, t):
                i = h * T + t
                V.reciprocal(recip[:], col(sums, t)).then_inc(s["recip_ready"], 1)
                dve.wait_ge(s["recip_ready"], i + 1)
                V.scalar_tensor_tensor(norm[:], col(rowmax, t), 0.5 * HALF * MASKED, recip[:], ALU.is_gt, ALU.mult).then_inc(s["norm_ready"], 1)
                dve.wait_ge(s["norm_ready"], i + 1)
                dve.wait_ge(s["av_done"], i + 1)
                V.scalar_tensor_tensor(sl(acc, t), ps[:, O_BANK, 0:D], norm[:], sl(acc, t), ALU.mult, ALU.add).then_inc(s["acc_done"], 1)

            with dve.Fori(0, H) as h:
                _, c0 = head_start(h)
                dve.wait_ge(s["wo_hi"], h + 1)
                V.scalar_tensor_tensor(wo_s[:, 1, :, :], wo_in, S_W, wo_s[:, 0, :, :], ALU.mult, ALU.subtract).then_inc(s["wo_free"], 1)
                for k in range(GROUPS):
                    if k == 12:
                        for c in range(3):
                            row_logits(h, 0, c)
                            row_max(h, 0, c)
                        row_shift(h, 0)
                    dve.wait_ge(s["proj_hi"], GROUPS * h + k + 1)
                    hi, src, scale = group_io(k, 0, c0)
                    lo, _, _ = group_io(k, 1, c0)
                    V.scalar_tensor_tensor(lo, src, scale, hi, ALU.mult, ALU.subtract).then_inc(s["proj_lo"], 1)
                with dve.Fori(0, T - 1) as t:
                    i = h * T + t
                    dve.wait_ge(s["exp_done"], i + 1)
                    row_logits(h, t + 1, 0)
                    row_max(h, t + 1, 0)
                    row_logits(h, t + 1, 1)
                    for g_ in range(3):
                        probs_lo(i, g_)
                    row_max(h, t + 1, 1)
                    row_logits(h, t + 1, 2)
                    row_max(h, t + 1, 2)
                    row_shift(h, t + 1)
                    gather_rows(h, t)
                for g_ in range(3):
                    probs_lo(h * T + T - 1, g_)
                gather_rows(h, T - 1)

            dve.wait_ge(s["acc_done"], T * H + 1)
            V.tensor_scalar(acc[:, :, :], acc[:, :, :], 1.0 / S_ACC, None, ALU.mult).then_inc(s["x1_ready"], 1)
            dve.wait_ge(s["x1_ready"], 1)
            layernorm("2", yn, s["yn_ready"])
            dve.wait_ge(s["yn_ready"], T)
            V.tensor_tensor(acc[:, :, :], acc[:, :, :], yn, ALU.add).then_inc(s["base_ready"], 1)

            V.tensor_scalar(ynsp[:, :, 0, :], yn, S_X, None, ALU.mult).then_inc(s["ynsp_hi"], 1)
            dve.wait_ge(s["ynsp_hi"], 1)
            V.scalar_tensor_tensor(ynsp[:, :, 1, :], yn, S_X, ynsp[:, :, 0, :], ALU.mult, ALU.subtract).then_inc(s["ynsp_lo"], 1)
            dve.wait_ge(s["gate_in"], 32)
            dve.wait_ge(s["gate_done"], 1)
            V.tensor_tensor(glog, ps[:, 6, 0:T * E].rearrange("p (t e) -> p t e", e=E),
                            bgbc.unsqueeze(1).to_broadcast([P, T, E]), ALU.add).then_inc(s["glog_ready"], 1)
            dve.wait_ge(s["glog_ready"], 1)
            for t in range(T):
                V.max(top8[:, t, :], glog[:, t, :]).then_inc(s["top8_ready"], 1)
            dve.wait_ge(s["top8_ready"], T)
            V.tensor_tensor(gap, top8[:, :, 1], top8[:, :, 0], ALU.subtract).then_inc(s["gap_ready"], 1)
            for t in range(T):
                V.max_index(idx8[:, t, :], top8[:, t, :], glog[:, t, :]).then_inc(s["idx_ready"], 1)
            dve.wait_ge(s["idx_ready"], T)
            V.tensor_copy(idxf, idx8).then_inc(s["idxf_ready"], 1)
            dve.wait_ge(s["route_consts"], 9)
            V.tensor_copy(iota_f, iota_i).then_inc(s["idxf_ready"], 1)
            V.tensor_copy(jb_f, jb_i).then_inc(s["idxf_ready"], 1)
            dve.wait_ge(s["idxf_ready"], 3)
            for k, one in enumerate((one1, one2)):
                V.tensor_tensor(one, iota_f.unsqueeze(1).to_broadcast([P, T, E]), idxf[:, :, k:k + 1].to_broadcast([P, T, E]),
                                ALU.is_equal).then_inc(s["onehot_ready"], 1)
            dve.wait_ge(s["onehot_ready"], 2)
            V.tensor_tensor(chosen[:, 0:T, :], one1, one2, ALU.add).then_inc(s["chosen_sum"], 1)
            dve.wait_ge(s["chosen_sum"], 1)
            V.tensor_tensor(chosen, chosen, rowok, ALU.mult).then_inc(s["chosen_ready"], 1)
            dve.wait_ge(s["expgap_ready"], 1)
            V.tensor_scalar(den, expgap, 1.0, None, ALU.add).then_inc(s["den_ready"], 1)
            dve.wait_ge(s["den_ready"], 1)
            V.reciprocal(gate[:, 0, :], den).then_inc(s["gate1_ready"], 1)
            dve.wait_ge(s["gate1_ready"], 1)
            V.tensor_tensor(gate[:, 1, :], expgap, gate[:, 0, :], ALU.mult).then_inc(s["gate_ready"], 1)
            rank = ps[:, 7, 0:(T + 1) * E].rearrange("p (t e) -> p t e", e=E)
            dve.wait_ge(s["rank_done"], 1)
            V.tensor_scalar(countsi, rank[:, T, :], float(P - 1), None, ALU.add).then_inc(s["countsi_ready"], 1)
            dve.wait_ge(s["countsi_ready"], 1)
            V.tensor_scalar(padi, countsi, -P, None, ALU.bitwise_and).then_inc(s["padi_ready"], 1)
            dve.wait_ge(s["padi_ready"], 1)
            V.tensor_copy(padf, padi).then_inc(s["padf_ready"], 1)
            dve.wait_ge(s["padf_ready"], 1)
            V.tensor_tensor_scan(ends, onesr, padf, 0.0, ALU.mult, ALU.add).then_inc(s["ends_ready"], 1)
            dve.wait_ge(s["ends_ready"], 1)
            V.tensor_tensor(base, ends, padf, ALU.subtract).then_inc(s["base_e_ready"], 1)
            dve.wait_ge(s["base_e_ready"], 1)
            V.tensor_tensor(slot_e, rank[:, 0:T, :], base.unsqueeze(1).to_broadcast([P, T, E]), ALU.add).then_inc(s["slot_e_ready"], 1)
            dve.wait_ge(s["slot_e_ready"], 1)
            for k, one in enumerate((one1, one2)):
                V.tensor_tensor(pick, one, slot_e, ALU.mult).then_inc(s["pick_ready"], 1)
                dve.wait_ge(s["pick_ready"], k + 1)
                V.tensor_reduce(slotf[:, k, :], pick, AX.X, ALU.add).then_inc(s["slotf_ready"], 1)
                dve.wait_ge(s["slotf_ready"], k + 1)
            V.tensor_copy(slot, slotf).then_inc(s["slot_ready"], 1)
            V.tensor_tensor(jcmp[0:1, :, :], jb_f[0:1, :].unsqueeze(2).to_broadcast([1, BLOCKS, E]),
                            ends[0:1, :].unsqueeze(1).to_broadcast([1, BLOCKS, E]), ALU.is_ge).then_inc(s["jcmp_ready"], 1)
            dve.wait_ge(s["jcmp_ready"], 1)
            V.tensor_reduce(jexp[0:1, :], jcmp[0:1, :, :], AX.X, ALU.add).then_inc(s["jexp_ready"], 1)
            dve.wait_ge(s["jexp_ready"], 1)
            V.tensor_scalar(block_expert[0:1, :], jexp[0:1, :], float(E - 1), None, ALU.min).then_inc(s["block_expert_ready"], 1)
            dve.wait_ge(s["block_expert_ready"], 1)

            def x_parts(j):
                dve.wait_ge(s["ex_T"], j + 1)
                V.tensor_copy(xT.rearrange("p s f n -> p (s f n)"), xt_bank).then_inc(s["ex_x"], 1)

            def h_parts(j):
                for half in range(2):
                    src = hid[:, 512 * half:512 * (half + 1)]
                    hi, lo = (hT[:, k, 4 * half:4 * half + 4, :].rearrange("p f n -> p (f n)") for k in range(2))
                    dve.wait_ge(s["gelu_done"], 2 * j + half + 1)
                    V.tensor_scalar(hi, src, S_H, None, ALU.mult).then_inc(s["ex_h_hi"], 1)
                    dve.wait_ge(s["ex_h_hi"], 2 * j + half + 1)
                    V.scalar_tensor_tensor(lo, src, S_H, hi, ALU.mult, ALU.subtract).then_inc(s["ex_h_lo"], 1)

            def y_rows(j):
                e = V.value_load(block_expert[0:1, bass.ds(j, 1)], min_val=0, max_val=E - 1)
                dve.wait_ge(s["ex_o"], j + 1)
                V.scalar_tensor_tensor(sl(xb, j), ps[:, Y_BANK, 0:D], 1.0 / (S_H * S_W), sl(b2bc, e),
                                       ALU.mult, ALU.add).then_inc(s["ys_ready"], 1)

            V.memset(dve_credit[:, 1:2], 0.0).then_inc(s["ex_h_lo"], 2)
            dve.wait_ge(s["b2_loaded"], 16)
            x_parts(0)
            x_parts(1)
            h_parts(0)
            with dve.Fori(1, BLOCKS - 1) as j:
                x_parts(j + 1)
                y_rows(j - 1)
                h_parts(j)
            y_rows(BLOCKS - 2)
            h_parts(BLOCKS - 1)
            y_rows(BLOCKS - 1)

            for t in range(T):
                rows = P if t < T - 1 else TAIL
                dve.wait_ge(gathered[t], 32)
                V.scalar_tensor_tensor(acc[0:rows, t, :], back[0:rows, 0, t, :], gate[0:rows, 0, t:t + 1], acc[0:rows, t, :],
                                       ALU.mult, ALU.add).then_inc(s["mix1"], 1)
                dve.wait_ge(s["mix1"], t + 1)
                V.scalar_tensor_tensor(acc[0:rows, t, :], back[0:rows, 1, t, :], gate[0:rows, 1, t:t + 1], acc[0:rows, t, :],
                                       ALU.mult, ALU.add).then_inc(s["out_ready"], 1)

        @block.tensor
        def _(pe):
            M = nc.tensor

            def three(dst, lhs, rhs, start, stop):
                for n, (a, b) in enumerate(((0, 0), (0, 1), (1, 0))):
                    last = M.matmul(dst, lhs(a), rhs(b), start=start and n == 0, stop=stop and n == 2)
                return last

            def transposed(src, ready, done):
                for k in range(TP + 1):
                    tiles = 2 if k < TP else 1
                    for j in range(tiles):
                        pe.wait_ge(ready, 2 * k + j + 1)
                        for ft in range(DT):
                            last = M.transpose(ps[:, k, (ft * tiles + j) * P:(ft * tiles + j + 1) * P],
                                               src[:, 2 * k + j, ft * P:(ft + 1) * P], ident[:])
                    last.then_inc(done, 1)

            pe.wait_ge(s["consts_ready"], 3)
            transposed(xn, s["xn_ready"], s["xT_done"])
            pe.wait_ge(s["b1_loaded"], 16)
            M.transpose(ps[:, 6, 0:E * FT], b1rows, ident[0:E * FT, 0:E * FT]).then_inc(s["b1_done"], 1)

            def project(h, k, first=False):
                w, dst_dt, half = (wk_s, wq_s, wv_s)[k // 4], k // 2 % 2, k % 2
                t0, _ = head_start(h)
                if first and k % 4 == 0:
                    pe.wait_ge(s["w_lo"], k + 4)
                if k >= 4:
                    pe.wait_ge(s["proj_lo"], GROUPS * h + k - 3)
                elif not first and k < 2:
                    pe.wait_ge(s["logits_done"], 3 * T * h)
                elif not first:
                    pe.wait_ge(s["acc_done"], T * h + 1)
                dst = pair(k)
                for j in range(4):
                    b = 4 * half + j
                    for ft in range(DT):
                        last = three(dst[:, j, 0:WIN], lambda a: w[:, a, ft, b * D + dst_dt * P:b * D + (dst_dt + 1) * P],
                                     lambda c: xnT[:, c, ft, bass.ds(t0, WIN)], ft == 0, ft == DT - 1)
                last.then_inc(s["proj_done"], 1)

            def project_out(h, k):
                if k < 14:
                    pe.wait_ge(s["proj_lo"], GROUPS * h + 12)
                else:
                    pe.wait_ge(s["logits_done"], 3 * T * h + 3)
                dst = pair(k)
                c0, n = PG[k - 12]
                for j in range(n):
                    at = PAD + (c0 + j) * P
                    for ft in range(DT):
                        last = three(dst[:, j, 0:D], lambda a: vT[:, a, ft, at:at + P], lambda c: wo_s[:, c, ft, :],
                                     ft == 0, ft == DT - 1)
                last.then_inc(s["proj_done"], 1)

            def scores(h, t, c, first=False):
                c0, w = CH[c]
                if not first:
                    pe.wait_ge(s["logits_done"], 3 * (h * T + t) + c - 2)
                at = t * P + PAD
                for ft in range(DT):
                    last = three(ps[:, S_BANK[c], 0:w], lambda a: qT[:, a, ft, bass.ds(at, P)] if not first else qT[:, a, ft, PAD:PAD + P],
                                 lambda b: kT[:, b, ft, PAD + c0:PAD + c0 + w], ft == 0, ft == DT - 1)
                last.then_inc(s["qk_done"], 1)

            def transposes(h, t, g_):
                i = h * T + t
                if g_ == 0:
                    pe.wait_ge(s["exp_done"], i + 1)
                c0, n = PG[g_]
                for j in range(n):
                    last = M.transpose(ps[:, T_BANK + g_, j * P:(j + 1) * P], prob[:, (c0 + j) * P:(c0 + j + 1) * P], ident[:])
                last.then_inc(s["t_done"], 1)

            def attend(h, t):
                i = h * T + t
                pe.wait_ge(s["acc_done"], i + 1)
                for g_, (c0, n) in enumerate(PG):
                    pe.wait_ge(s["p_lo"], 3 * i + g_ + 1)
                    for c in range(c0, c0 + n):
                        k = P if c < T - 1 else TAIL
                        last = three(ps[:, O_BANK, 0:D], lambda a: probT[0:k, a, c * P:(c + 1) * P],
                                     lambda b: vo[0:k, b, c, :], c == 0, c == T - 1)
                last.then_inc(s["av_done"], 1)

            pe.wait_ge(s["xT_lo"], TP + 1)
            pe.wait_ge(s["b1_ready"], 1)
            pe.wait_ge(s["pads_ready"], 2)
            def head(h, first=False, last=False):
                for k in range(2, 12):
                    project(h, k, first)
                pe.wait_ge(s["proj_lo"], GROUPS * h + 10)
                for c in range(3):
                    scores(h, 0, c, first=True)
                pe.wait_ge(s["wo_free"], h + 2)
                for k in range(12, 15):
                    project_out(h, k)
                with pe.Fori(0, T - 1) as t:
                    scores(h, t + 1, 0)
                    scores(h, t + 1, 1)
                    pe.wait_ge(s["proj_lo"], GROUPS * h + GROUPS)
                    for g_ in range(3):
                        transposes(h, t, g_)
                    scores(h, t + 1, 2)
                    attend(h, t)
                if not last:
                    project(h + 1, 0)
                for g_ in range(3):
                    transposes(h, T - 1, g_)
                if not last:
                    project(h + 1, 1)
                attend(h, T - 1)

            project(0, 0, True)
            project(0, 1, True)
            head(0, first=True)
            with pe.Fori(1, H - 1) as h:
                head(h)
            head(H - 1, last=True)

            pe.wait_ge(s["acc_done"], T * H + 1)
            transposed(yn, s["yn_ready"], s["ynT_done"])
            pe.wait_ge(s["gate_in"], 32)
            pe.wait_ge(s["ynT_ready"], TP + 1)
            for t in range(T):
                for ft in range(DT):
                    last = M.matmul(ps[:, 6, t * E:(t + 1) * E], ynT[:, ft, t * P:(t + 1) * P], wg_sb[:, ft, :],
                                    start=ft == 0, stop=ft == DT - 1)
            last.then_inc(s["gate_done"], 1)
            pe.wait_ge(s["route_consts"], 9)
            pe.wait_ge(s["chosen_ready"], 1)
            rank = ps[:, 7, 0:(T + 1) * E].rearrange("p (t e) -> p t e", e=E)
            M.matmul(rank, ones, chosen[:, T:T + 1, :].to_broadcast([P, T + 1, E]), start=True, stop=False)
            for t in range(T):
                M.matmul(rank[:, t + 1:T + 1, :], ones, chosen[:, t:t + 1, :].to_broadcast([P, T - t, E]),
                         start=False, stop=False, skip_group_check=True)
            last = M.matmul(rank, tri, chosen, start=False, stop=True)
            last.then_inc(s["rank_done"], 1)

            def block_T(j):
                if not isinstance(j, int) or j > 0:
                    pe.wait_ge(s["ex_x"], j)
                for q in range(2 * DT):
                    last = M.transpose(xt_bank[:, q * P:(q + 1) * P],
                                       xb16[:, bass.ds(j, 1), q * P:(q + 1) * P].rearrange("p j n -> p (j n)"), ident16[:])
                last.then_inc(s["ex_T"], 1)

            def block_H(j, e):
                pe.wait_ge(s["experts_ready"], e + 1)
                pe.wait_ge(s["ex_x"], j + 1)
                for half in range(2):
                    if not isinstance(j, int) or j > 0:
                        pe.wait_ge(s["gelu_done"], 2 * j - 1 + half)
                    for ft in range(4 * half, 4 * half + 4):
                        for k in range(DT):
                            last = three(flat[:, 512 * H_BANK + ft * P:512 * H_BANK + (ft + 1) * P],
                                         lambda a: w1_s[a][:, bass.ds(e, 1), k, ft * P:(ft + 1) * P].rearrange("p e n -> p (e n)"),
                                         lambda b: xT[:, b, k, :], k == 0, k == DT - 1)
                    last.then_inc(s["ex_h"], 1)

            def block_O(j, e):
                if not isinstance(j, int) or j > 0:
                    pe.wait_ge(s["ys_ready"], j)
                for ft in range(FT):
                    if ft % 4 == 0:
                        pe.wait_ge(s["ex_h_lo"], 2 * j + ft // 4 + 3)
                    last = three(ps[:, Y_BANK, 0:D], lambda a: hT[:, a, ft, :],
                                 lambda b: w2_s[b][:, bass.ds(e, 1), ft, :].rearrange("p e n -> p (e n)"), ft == 0, ft == FT - 1)
                last.then_inc(s["ex_o"], 1)

            def expert(j):
                return M.value_load(block_expert[0:1, bass.ds(j, 1)], min_val=0, max_val=E - 1)

            pe.wait_ge(s["block_expert_ready"], 1)
            pe.wait_ge(xb_in[0], 16)
            block_T(0)
            block_H(0, expert(0))
            for q in xb_in[1:]:
                pe.wait_ge(q, 16)
            block_T(1)
            with pe.Fori(1, BLOCKS - 1) as j:
                block_H(j, expert(j))
                block_T(j + 1)
                block_O(j - 1, expert(j - 1))
            block_H(BLOCKS - 1, expert(BLOCKS - 1))
            block_O(BLOCKS - 2, expert(BLOCKS - 2))
            block_O(BLOCKS - 1, expert(BLOCKS - 1))


_INS = ["x", "adj", "L0_gnn_Wq", "L0_gnn_Wk", "L0_gnn_Wv", "L0_gnn_Wout", "L0_ffn_Wg", "L0_ffn_bg",
        "L0_ffn_W1", "L0_ffn_b1", "L0_ffn_W2", "L0_ffn_b2"]


def kernel(**inputs):
    import numpy as _np
    import concourse.bacc as _bacc
    from concourse import mybir as _mybir
    from concourse.bass_utils import run_bass_kernel_spmd as _run

    nc = _bacc.Bacc("TRN2", target_bir_lowering=False, num_devices=1)
    arrays, args = {}, []
    for name in _INS:
        a = _np.ascontiguousarray(inputs[name])
        arrays[f"in_{name}_dram"] = a
        args.append(nc.dram_tensor(f"in_{name}_dram", a.shape, _mybir.dt.from_np(a.dtype), kind="ExternalInput").ap())
    args.append(nc.dram_tensor("out_0_dram", (N, D), F32, kind="ExternalOutput").ap())
    args.append(nc.dram_tensor("w_split_dram", (E * P, 4, 2048), F16, kind="Internal").ap())
    args.append(nc.dram_tensor("xs_dram", (BLOCKS * P, 2 * D), F16, kind="Internal").ap())
    args.append(nc.dram_tensor("ys_dram", (BLOCKS * P, D), F32, kind="Internal").ap())
    build(nc, *args)
    r = _run(nc, [arrays], core_ids=[0])
    return r.results[0]["out_0_dram"]
```

```python
from contextlib import ExitStack

import concourse.bass as bass
from concourse import mybir

ALU = mybir.AluOpType
ACT = mybir.ActivationFunctionType
AX = mybir.AxisListType
F32 = mybir.dt.float32
F16 = mybir.dt.float16
I32 = mybir.dt.int32
U32 = mybir.dt.uint32

P = 128
N = 1354
D = 256
H = 8
E = 8
FF = 1024
DT = D // P
FT = FF // P
T = (N + P - 1) // P
TAIL = N - (T - 1) * P
TP = T // 2
NP = T * P
BLOCKS = (2 * N + E * (P - 1)) // P
WIN = N // 8 + 2
PAD = 16
QW = PAD + NP
CH = [(0, 512), (512, 512), (1024, N - 1024)]
PG = [(0, 4), (4, 4), (8, T - 8)]
XR, YR = 4, 4
QUADS = (BLOCKS - 1) // 4
GROUPS = 15
EPS = 1e-5

S_X = 2.0 ** 8
S_W = 2.0 ** 9
S_Q = 2.0 ** 5
S_V = 2.0 ** 8
S_P = 2.0 ** 12
S_H = 2.0 ** 6
S_LOGIT = S_Q * S_Q * 16.0
HALF = 0.5
S_ACC = S_P * S_V
S_G = 2.0 ** 10
assert BLOCKS == 4 * QUADS + 1
MASKED = -1.0e6


class Map:

    def __init__(self, arena):
        self.arena, self.at = arena, 0

    def take(self, cols, dt):
        size = 4 if dt in (F32, I32, U32) else 2
        view = self.arena[:, self.at // 2:(self.at + cols * size) // 2]
        self.at += cols * size
        return view if dt == F16 else view.bitcast(dt)


def build(nc, x, adj, Wq, Wk, Wv, Wout, Wg, bg, W1, b1, W2, b2, out, w_split, yn_rows, mix):
    with ExitStack() as ctx:
        def sb(name, shape, dt):
            return ctx.enter_context(nc.sbuf_tensor(name, shape, dt))

        def sem(name):
            return ctx.enter_context(nc.semaphore(name))

        ARENA = 198528 // 2
        arena = sb("arena", [P, ARENA], F16)
        acc = sb("acc", [P, T, D], F32)
        ident = sb("ident", [P, P], F32)
        ident16 = sb("ident16", [P, P], F16)
        wscale = sb("wscale", [P, 1], F32)
        zero = sb("zero", [P, 1], F32)
        b1T = sb("b1T", [P, E * FT], F32)
        sums = sb("sums", [P, T], F32)
        rowmax = sb("rowmax", [P, T], F32)
        chunkmax = sb("chunkmax", [P, 3], F32)
        pool_credit = sb("pool_credit", [P, 1], F32)
        dve_credit = sb("dve_credit", [P, 2], F32)
        shift = sb("shift", [P, 1], F32)
        act_dummy = sb("act_dummy", [P, 1], F32)
        recip = sb("recip", [P, 1], F32)
        norm = sb("norm", [P, 1], F32)
        stats = sb("stats", [P, T, 6], F32)
        meanvar = sb("meanvar", [P, T, 2], F32)
        std = sb("std", [P, T], F32)
        rstd = sb("rstd", [P, T], F32)

        m = Map(arena)
        wqkv = [m.take(2 * DT * H * D, F16).rearrange("p (s f n) -> p s f n", s=2, f=DT) for _ in range(3)]
        wk_s, wq_s, wv_s = wqkv
        xnT = m.take(2 * DT * NP, F16).rearrange("p (s f n) -> p s f n", s=2, f=DT)
        vT = m.take(2 * DT * QW, F16).rearrange("p (s f n) -> p s f n", s=2, f=DT)
        kT = m.take(2 * DT * QW, F16).rearrange("p (s f n) -> p s f n", s=2, f=DT)
        at_q = m.at
        qT = m.take(2 * DT * QW, F16).rearrange("p (s f n) -> p s f n", s=2, f=DT)
        m2 = Map(arena)
        m2.at = at_q
        xn = m2.take(T * D, F32).rearrange("p (t d) -> p t d", d=D)
        vo = m.take(2 * T * D, F16).rearrange("p (s t d) -> p s t d", s=2, d=D)
        wo_s = m.take(2 * DT * D, F16).rearrange("p (s f n) -> p s f n", s=2, f=DT)
        wo_in = m.take(DT * D, F32).rearrange("p (f n) -> p f n", f=DT)
        bias = m.take(T * N, F32).rearrange("p (t n) -> p t n", n=N)
        logits = m.take(N, F32)
        prob = m.take(NP, F32)
        probT = m.take(2 * NP, F16).rearrange("p (s n) -> p s n", s=2)
        at_stage = m.at
        stage = m.take(3 * 1024, F32).rearrange("p (s n) -> p s n", s=3)
        assert m.at <= 2 * ARENA, m.at
        split_out = stage[:, 2, :].bitcast(F16).rearrange("p (s n) -> p s n", s=2)
        b1rows = logits[0:E * FT, 0:P]
        masked = stage[:, 0:2, :].rearrange("p s n -> p (s n)")[:, 0:N]

        f = Map(arena)
        we = f.take(E * 8192, F16).rearrange("p (e n) -> p e n", e=E)
        w1_s = [we[:, :, 2048 * s:2048 * (s + 1)].rearrange("p e (f n) -> p e f n", f=DT) for s in range(2)]
        w2_s = [we[:, :, 4096 + 2048 * s:4096 + 2048 * (s + 1)].rearrange("p e (f n) -> p e f n", f=FT)
                for s in range(2)]
        f_x = f.take(T * 2 * D, F16)
        ynT = f_x.rearrange("p (t s f n) -> p t s f n", t=T, s=2, f=DT)
        xb = f_x[:, 0:XR * 2 * D].rearrange("p (j n) -> p j n", j=XR)
        yb = f_x[:, XR * 2 * D:(XR + YR) * 2 * D].bitcast(F32).rearrange("p (j d) -> p j d", j=YR)
        yn = f.take(T * D, F32).rearrange("p (t d) -> p t d", d=D)
        ynsp = f.take(T * 2 * D, F16).rearrange("p (t s d) -> p t s d", s=2, d=D)
        b2bc = f.take(E * D, F32).rearrange("p (e d) -> p e d", d=D)
        f2 = Map(arena)
        f2.at = f.at
        hid = f.take(FF, F32)
        hT = f.take(2 * FF, F16).rearrange("p (s f n) -> p s f n", s=2, f=FT)
        xT = f.take(2 * D, F16).rearrange("p (s f n) -> p s f n", s=2, f=DT)
        row_hot = f2.take(2 * T * P, F16).rearrange("p (k t n) -> p k t n", k=2, t=T)
        assert f2.at <= f.at
        block_hot = f.take(2 * T * BLOCKS, F16).rearrange("p (k t j) -> p k t j", k=2, t=T)
        block_id = f.take(2 * T * BLOCKS, F16).rearrange("p (k t j) -> p k t j", k=2, t=T)
        f.at = max(f.at, at_stage)
        wg_sb = f.take(DT * E, F32).rearrange("p (f e) -> p f e", f=DT)
        wg_s = f.take(2 * DT * E, F16).rearrange("p (s f e) -> p s f e", s=2, f=DT)
        bgbc = f.take(E, F32)
        rowok = f.take(T * E, F32).rearrange("p (t e) -> p t e", e=E)
        chosen = f.take((T + 1) * E, F16).rearrange("p (t e) -> p t e", e=E)
        tri = f.take(P, F16)
        ones = f.take(P, F16)
        onesr = f.take(E, F32)
        iota_i = f.take(P, I32)
        iota_f = f.take(P, F32)
        jb_i = f.take(BLOCKS, I32)
        jb_f = f.take(BLOCKS, F32)
        ids_i = f.take(T + 1, I32)
        ids = f.take(T + 1, F32)
        glog = f.take(T * E, F32).rearrange("p (t e) -> p t e", e=E)
        top8 = f.take(T * E, F32).rearrange("p (t e) -> p t e", e=E)
        idx8 = f.take(T * E, U32).rearrange("p (t e) -> p t e", e=E)
        idxf = f.take(T * E, F32).rearrange("p (t e) -> p t e", e=E)
        one1 = f.take(T * E, F32).rearrange("p (t e) -> p t e", e=E)
        one2 = f.take(T * E, F32).rearrange("p (t e) -> p t e", e=E)
        both = f.take(T * E, F32).rearrange("p (t e) -> p t e", e=E)
        slot_e = f.take(T * E, F32).rearrange("p (t e) -> p t e", e=E)
        pick = f.take(T * E, F32).rearrange("p (t e) -> p t e", e=E)
        slotf = f.take(2 * T, F32).rearrange("p (k t) -> p k t", k=2)
        sloti = f.take(2 * T, I32).rearrange("p (k t) -> p k t", k=2)
        rowi = f.take(2 * T, I32).rearrange("p (k t) -> p k t", k=2)
        rowf = f.take(2 * T, F32).rearrange("p (k t) -> p k t", k=2)
        blockf = f.take(2 * T, F32).rearrange("p (k t) -> p k t", k=2)
        gate = f.take(2 * T, F32).rearrange("p (k t) -> p k t", k=2)
        gate_s = f.take(2 * 2 * T, F16).rearrange("p (s k t) -> p s k t", s=2, k=2)
        gap = f.take(T, F32)
        expgap = f.take(T, F32)
        den = f.take(T, F32)
        countsi = f.take(E, I32)
        padi = f.take(E, I32)
        padf = f.take(E, F32)
        ends = f.take(E, F32)
        base = f.take(E, F32)
        block_gate = f.take(2 * 2 * T * BLOCKS, F16).rearrange("p (s k t j) -> p s k t j", s=2, k=2, t=T)
        spare = f.take(BLOCKS, F32)
        token = f.take(BLOCKS, U32)
        slot_gate = f.take(BLOCKS, F32)
        jcmp = f.take(BLOCKS * E, F32).rearrange("p (j e) -> p j e", e=E)
        jexp = f.take(BLOCKS, F32)
        jword = f.take(QUADS, F32)
        block_expert = f.take(QUADS, I32)
        assert f.at <= 2 * ARENA, f.at

        ps = ctx.enter_context(nc.psum_tensor("ps", [P, 8, 512], F32))
        flat = ps[:, :, :].rearrange("p b n -> p (b n)")
        S_BANK = (6, 7, 5)
        T_BANK, O_BANK = 1, 0
        xt_bank = ps[:, 0, 0:D].bitcast(F16)
        ynT_ps = [ps[:, b, 0:D].bitcast(F16) for b in range(4)]
        H_BANK, Y_BANK = 1, 3
        glog_ps = ps[:, 6, 0:T * E].rearrange("p (t e) -> p t e", e=E)
        rank = ps[:, 7, 0:(T + 1) * E].rearrange("p (t e) -> p t e", e=E)
        token_ps, gate_ps = ps[:, 4, 0:BLOCKS], ps[:, 5, 0:BLOCKS]

        names = """consts_ready x_tail_zero x_loaded b1_loaded stats_done meanvar_done var_done std_done rstd_done
            xn_ready xT_done xT_hi xT_lo b1_done b1_ready w_loaded0 w_loaded1 w_loaded2 w_hi w_lo
            masks_made masks_ready pads_ready prob_pad
            wo_free wo_loaded wo_hi wo_ready proj_done proj_hi proj_lo
            qk_done logits_done chunkmax_done rowmax_ready shift_ready exp_done t_done p_hi p_lo av_done recip_ready norm_ready acc_done
            stage_free piece_loaded0 piece_loaded1 piece_hi piece_scaled piece_split piece_stored
            stats2_done meanvar2_done var2_done std2_done rstd2_done yn_ready ynsp_hi ynsp_lo ynT_done ynT_ready
            gate_in wg_hi wg_lo gate_done glog_ready top8_ready idx_ready idxf_ready gap_ready expgap_ready den_ready gate1_ready
            gate2_ready gate_ready onehot_ready chosen_sum chosen_ready rank_done countsi_ready padi_ready padf_ready ends_ready
            base_e_ready slot_e_ready pick_ready slotf_ready sloti_ready rowi_ready rowf_ready blockf_ready
            row_hot_ready block_hot_ready block_id_ready token_done spare_ready token_ready
            gate_hi gate_lo block_gate_ready slot_gate_done slot_gate_ready
            jcmp_ready jexp_ready jmin_ready block_expert_ready route_ints route_consts
            base_ready yn_stored base_stored b2_loaded experts_ready x_in ex_T ex_x ex_h gelu_done ex_h_hi ex_h_lo ex_o
            y_sum ys_ready mixed out_stored""".split()
        s = {n: sem(n) for n in names}
        expert_loaded = [sem(f"expert_loaded{e}") for e in range(E)]

        def head_start(h):
            return 169 * h + h // 4, PAD - (2 * h - 8 * (h // 4))

        assert N // 8 == 169 and N % 8 == 2
        PAIR = (4, 6, 2, 0) * 3 + (2, 0, 4)

        def pair(k):
            b = PAIR[k]
            return ps[:, b:b + 2, :].rearrange("p b (j n) -> p (b j) n", j=2)

        def group_io(k, part, c0):
            if k >= 12:
                a, n = PG[k - 12]
                return vo[:, part, a:a + n, :], pair(k)[:, 0:n, :], S_V / (S_Q * S_W)
            buf, q = (kT, qT, vT)[k // 4], k % 4
            rows = buf[:, part, q // 2, bass.ds(c0, 8 * WIN)].rearrange("p (t b) -> p b t", b=8)
            return rows[:, 4 * (q % 2):4 * (q % 2) + 4, :], pair(k)[:, :, 0:WIN], S_Q / (S_X * S_W)

        def col(buf, t):
            return buf[:, bass.ds(t, 1)]

        def sl(buf, t):
            return buf[:, bass.ds(t, 1), :].rearrange("p t n -> p (t n)")

        W1r = W1.rearrange("e k n -> (e k) n")
        W2r = W2.rearrange("e k n -> (e k) n")
        ADJ = [(0, 1), (1, 5), (5, T - 1), (T - 1, T)]
        adj_in = [sem(f"adj_in{k}") for k in range(len(ADJ))]

        def experts_of(eng, i):
            word = eng.value_load(block_expert[0:1, bass.ds(i, 1)], min_val=0, max_val=E ** 5 - 1)
            return [eng.snap((word // E ** u) % E, min_val=0, max_val=E - 1) for u in range(5)]

        def token_rows(dram, view):
            left = N + P - NP
            return ((dram[0:NP, :].rearrange("(t p) d -> p t d", p=P), view), (dram[NP:N + P, :], view[0:left, 0, :]))

        block = ctx.enter_context(nc.Block())

        @block.sync
        def _(sp):
            sp.wait_ge(s["x_tail_zero"], 1)
            sp.dma_start(acc[:, 0:T - 1, :], x[0:(T - 1) * P, :].rearrange("(t p) d -> p t d", p=P)).then_inc(s["x_loaded"], 16)
            sp.dma_start(acc[0:TAIL, T - 1, :], x[(T - 1) * P:N, :]).then_inc(s["x_loaded"], 16)
            sp.dma_start(b1rows, b1.rearrange("e (f p) -> (e f) p", p=P)).then_inc(s["b1_loaded"], 16)
            adj_after = {6: 0, 10: 1}
            c = 0
            for w in (Wk, Wq, Wv):
                for ft in range(DT):
                    for half in range(2):
                        if c >= 3:
                            sp.wait_ge(s["w_lo"], c - 2)
                        sp.dma_start(stage[:, c % 3, :], w[ft * P:(ft + 1) * P, half * 1024:(half + 1) * 1024]
                                     ).then_inc(s[f"w_loaded{c % 3}"], 16)
                        c += 1
                        if c in adj_after:
                            a, b = ADJ[adj_after[c]]
                            sp.dma_start(bias[:, a:b, :], adj[a * P:b * P, :].rearrange("(t p) n -> p t n", p=P)
                                         ).then_inc(adj_in[adj_after[c]], 16)

            def wout(h):
                sp.wait_ge(s["wo_free"], h + 1)
                sp.dma_start(wo_in, Wout[bass.ds(h * D, D), :].rearrange("(f p) n -> p f n", p=P)).then_inc(s["wo_loaded"], 16)

            def expert_weights(e):
                for q in range(4):
                    sp.wait_ge(s["stage_free"], e * 4 + q + 1)
                    if q < 2:
                        src = W1r[bass.ds(e * D + q * P, P), :]
                        dst = stage[:, q % 2, :]
                    else:
                        src = W2r[bass.ds(e * FF + (q - 2) * 512, 512), :].rearrange("(f p) n -> p f n", p=P)
                        dst = stage[:, q % 2, :].rearrange("p (f n) -> p f n", n=D)
                    sp.dma_start(dst, src).then_inc(s[f"piece_loaded{q % 2}"], 16)

            wout(0)
            a, b = ADJ[2]
            sp.dma_start(bias[:, a:b, :], adj[a * P:b * P, :].rearrange("(t p) n -> p t n", p=P)).then_inc(adj_in[2], 16)
            sp.wait_ge(s["masks_made"], 1)
            sp.dma_start(bias[0:TAIL, T - 1, :], adj[(T - 1) * P:N, :]).then_inc(adj_in[3], 16)
            expert_weights(0)
            with sp.Fori(1, H) as h:
                wout(h)
                expert_weights(h)
            sp.wait_ge(s["piece_stored"], 16 * 4 * E)
            sp.dma_start(wg_sb, Wg.rearrange("(f p) e -> p f e", p=P)).then_inc(s["gate_in"], 16)
            sp.dma_start(bgbc, bg.partition_broadcast(P)).then_inc(s["gate_in"], 16)

            def expert_in(e):
                sp.dma_start(we[:, e, :].rearrange("p (k n) -> p k n", k=4), w_split[e * P:(e + 1) * P, :, :]).then_inc(expert_loaded[e], 16)

            def experts_in(es):
                for e in es:
                    sp.wait_ge(expert_loaded[e], 16)
                    sp.sem_inc(s["experts_ready"], 1)

            sp.wait_ge(s["proj_done"], GROUPS * H)
            for e in range(4):
                expert_in(e)
            experts_in(range(4))
            sp.wait_ge(s["acc_done"], T * H + 1)
            sp.dma_start(b2bc, b2.partition_broadcast(P)).then_inc(s["b2_loaded"], 16)
            expert_in(4)
            expert_in(5)
            sp.wait_ge(s["ynsp_lo"], T)
            for rows, view in token_rows(yn_rows, ynsp.rearrange("p t s d -> p t (s d)")):
                sp.dma_start(rows, view).then_inc(s["yn_stored"], 16)
            expert_in(6)
            sp.wait_ge(s["base_ready"], 1)
            for rows, view in token_rows(mix, acc[:, :, :]):
                sp.dma_start(rows, view).then_inc(s["base_stored"], 16)
            expert_in(7)
            experts_in(range(4, E))
            sp.wait_ge(s["mixed"], 16 * BLOCKS)
            sp.dma_start(out[:, :], mix[0:N, :]).then_inc(s["out_stored"], 16)
            sp.wait_ge(s["out_stored"], 16)

        @block.gpsimd
        def _(pool):
            gp = nc.gpsimd
            gp.memset(ident[:], 0.0).then_inc(s["consts_ready"], 1)
            pool.wait_ge(s["consts_ready"], 1)
            gp.affine_select(out=ident[:], in_=ident[:], compare_op=ALU.not_equal, fill=1.0, base=0,
                             pattern=[[-1, P]], channel_multiplier=1).then_inc(s["consts_ready"], 1)
            pool.wait_ge(s["consts_ready"], 2)
            gp.tensor_scalar(ident16[:], ident[:], 1.0, None, ALU.mult).then_inc(s["consts_ready"], 1)
            gp.memset(wscale[:], S_W).then_inc(s["consts_ready"], 1)
            gp.memset(zero[:], 0.0).then_inc(s["consts_ready"], 1)
            gp.memset(prob[:, N:NP], 0.0).then_inc(s["prob_pad"], 1)
            gp.memset(bias[:, T - 1, :], 0.0).then_inc(s["masks_made"], 1)
            pool.wait_ge(s["w_lo"], 12)
            for k, (a, b) in enumerate(ADJ):
                pool.wait_ge(adj_in[k], 16)
                for t in range(a, b):
                    row = bias[:, t, :]
                    gp.tensor_scalar(masked, row, 0.0, HALF * MASKED, ALU.is_equal, ALU.mult).then_inc(s["masks_made"], 1)
                    pool.wait_ge(s["masks_made"], t + 2)
                    gp.tensor_tensor(row, row, masked, ALU.add).then_inc(s["masks_ready"], 1)
                    pool.wait_ge(s["masks_ready"], t + 1)
            pool.wait_ge(s["consts_ready"], 5)
            gp.memset(pool_credit[:], 0.0).then_inc(s["stage_free"], 2)
            with pool.Fori(0, E) as e:
                for q in range(4):
                    n = e * 4 + q
                    src = stage[:, q % 2, :]
                    pool.wait_ge(s[f"piece_loaded{q % 2}"], 32 * e + 16 * (q // 2) + 16)
                    gp.tensor_tensor(src, src, wscale[:].to_broadcast([P, 1024]), ALU.mult).then_inc(s["piece_scaled"], 1)
                    pool.wait_ge(s["piece_scaled"], n + 1)
                    gp.tensor_tensor(split_out[:, 0, :], src, zero[:].to_broadcast([P, 1024]), ALU.add).then_inc(s["piece_hi"], 1)
                    pool.wait_ge(s["piece_hi"], n + 1)
                    gp.tensor_tensor(split_out[:, 1, :], src, split_out[:, 0, :], ALU.subtract).then_inc(s["stage_free"], 1)
                    pool.wait_ge(s["stage_free"], n + 3)
                    a, c = 2 * (q // 2), (q % 2) * 1024
                    dst = w_split[bass.ds(e * P, P), a:a + 2, c:c + 1024]
                    gp.dma_start(dst, split_out).then_inc(s["piece_stored"], 16)
                    pool.wait_ge(s["piece_stored"], 16 * n + 16)
            pool.wait_ge(s["piece_stored"], 16 * 4 * E)
            gp.iota(iota_i, pattern=[[1, P]], base=0, channel_multiplier=0).then_inc(s["route_ints"], 1)
            gp.iota(jb_i, pattern=[[P, BLOCKS]], base=0, channel_multiplier=0).then_inc(s["route_ints"], 1)
            gp.iota(ids_i[:, 0:T], pattern=[[P, T]], base=1, channel_multiplier=1).then_inc(s["route_ints"], 1)
            gp.iota(ids_i[:, T:T + 1], pattern=[[1, 1]], base=N + 1, channel_multiplier=1).then_inc(s["route_ints"], 1)
            gp.memset(chosen, 0.0).then_inc(s["route_ints"], 1)
            gp.memset(rowok, 1.0).then_inc(s["route_ints"], 1)
            gp.memset(tri, 1.0).then_inc(s["route_ints"], 1)
            gp.memset(ones, 1.0).then_inc(s["route_consts"], 1)
            gp.memset(onesr, 1.0).then_inc(s["route_consts"], 1)
            pool.wait_ge(s["route_ints"], 7)
            gp.tensor_scalar(iota_f, iota_i, 1.0, None, ALU.mult).then_inc(s["route_consts"], 1)
            gp.tensor_scalar(jb_f, jb_i, 1.0, None, ALU.mult).then_inc(s["route_consts"], 1)
            gp.tensor_scalar(ids, ids_i, 1.0, None, ALU.mult).then_inc(s["route_consts"], 1)
            gp.affine_select(out=rowok, in_=rowok, compare_op=ALU.is_ge, fill=0.0, base=N - 1,
                             pattern=[[-P, T], [0, E]], channel_multiplier=-1).then_inc(s["route_consts"], 1)
            gp.affine_select(out=tri, in_=tri, compare_op=ALU.is_ge, fill=0.0, base=-1,
                             pattern=[[1, P]], channel_multiplier=-1).then_inc(s["route_consts"], 1)
            pool.wait_ge(s["route_consts"], 7)
            gp.tensor_tensor(ids[:, 0:T], ids[:, 0:T], rowok[:, :, 0], ALU.mult).then_inc(s["route_consts"], 1)
            def gather(j):
                gp.indirect_dma_start(xb[:, j % XR, :], None, yn_rows[:, :],
                                      bass.IndirectOffsetOnAxis(ap=token[:, j:j + 1], axis=0)).then_inc(s["x_in"], 16)

            pool.wait_ge(s["token_ready"], 1)
            pool.wait_ge(s["yn_stored"], 32)
            pool.wait_ge(s["gate_done"], 1)
            for j in range(XR):
                if j > 0:
                    pool.wait_ge(s["x_in"], 16 * j)
                gather(j)
            pool.wait_ge(s["base_stored"], 32)
            for j in range(BLOCKS):
                if j + XR < BLOCKS:
                    pool.wait_ge(s["ex_T"], j + 1)
                    pool.wait_ge(s["x_in"], 16 * (j + XR))
                    gather(j + XR)
                pool.wait_ge(s["ys_ready"], j + 1)
                if j > 0:
                    pool.wait_ge(s["mixed"], 16 * j)
                gp.indirect_dma_start(mix[:, :], bass.IndirectOffsetOnAxis(ap=token[:, j:j + 1], axis=0), yb[:, j % YR, :], None,
                                      compute_op=ALU.add).then_inc(s["mixed"], 16)

        @block.scalar
        def _(act):
            A = nc.scalar

            def copy(dst, src, scale):
                return A.activation(dst, src, ACT.Copy, scale=scale)

            act.wait_ge(s["var_done"], 1)
            A.activation(std[:], std[:], ACT.Sqrt).then_inc(s["std_done"], 1)
            for k in range(TP + 1):
                w = 2 * P if k < TP else P
                act.wait_ge(s["xT_done"], k + 1)
                copy(xnT[:, 0, :, 2 * P * k:2 * P * k + w], ps[:, k, 0:2 * w].rearrange("p (f n) -> p f n", f=DT), S_X
                     ).then_inc(s["xT_hi"], 1)
            act.wait_ge(s["consts_ready"], 5)
            A.activation(act_dummy[:], zero[:], ACT.Exp)

            def weights_hi(chunks):
                for c in chunks:
                    act.wait_ge(s[f"w_loaded{c % 3}"], 16 * (c // 3 + 1))
                    copy(wqkv[c // 4][:, 0, (c // 2) % 2, (c % 2) * 1024:(c % 2 + 1) * 1024], stage[:, c % 3, :], S_W).then_inc(s["w_hi"], 1)

            def probs(h, t):
                i = h * T + t
                act.wait_ge(s["shift_ready"], i + 1)
                A.activation(prob[:, 0:N], logits, ACT.Exp, bias=shift[:], scale=1.0 / HALF,
                             accum_out=col(sums, t)).then_inc(s["exp_done"], 1)

            def probs_hi(i):
                for g_, (c0, k) in enumerate(PG):
                    act.wait_ge(s["t_done"], 3 * i + g_ + 1)
                    copy(probT[:, 0, c0 * P:(c0 + k) * P], ps[:, T_BANK + g_, 0:k * P], S_P).then_inc(s["p_hi"], 1)

            def head(h, first=False):
                _, c0 = head_start(h)
                for k in range(GROUPS):
                    if k == 4 and first:
                        weights_hi(range(8, 12))
                    if k == 8:
                        act.wait_ge(s["wo_loaded"], 16 * h + 16)
                        copy(wo_s[:, 0, :, :], wo_in, S_W).then_inc(s["wo_hi"], 1)
                    if k == 12:
                        probs(h, 0)
                    act.wait_ge(s["proj_done"], GROUPS * h + k + 1)
                    dst, src, scale = group_io(k, 0, c0)
                    copy(dst, src, scale).then_inc(s["proj_hi"], 1)
                with act.Fori(0, T - 1) as t:
                    i = h * T + t
                    probs_hi(i)
                    probs(h, t + 1)
                probs_hi(h * T + T - 1)

            weights_hi(range(8))
            head(0, first=True)
            with act.Fori(1, H) as h:
                head(h)
            A.activation(act_dummy[:], zero[:], ACT.Sqrt)

            act.wait_ge(s["gate_in"], 32)
            copy(wg_s[:, 0, :, :], wg_sb, S_W).then_inc(s["wg_hi"], 1)
            act.wait_ge(s["var2_done"], 1)
            A.activation(std[:], std[:], ACT.Sqrt).then_inc(s["std2_done"], 1)
            A.activation(act_dummy[:], zero[:], ACT.Exp)
            for t in range(T + 2):
                if t < T:
                    act.wait_ge(s["yn_ready"], t + 1)
                    copy(ynsp[:, t, 0, :], yn[:, t, :], S_X).then_inc(s["ynsp_hi"], 1)
                if t >= 2:
                    act.wait_ge(s["ynT_done"], t - 1)
                    copy(ynT[:, t - 2, :, :, :].rearrange("p s f n -> p (s f n)"), ynT_ps[(t - 2) % 4], 1.0).then_inc(s["ynT_ready"], 1)
            act.wait_ge(s["gap_ready"], 1)
            A.activation(expgap, gap, ACT.Exp).then_inc(s["expgap_ready"], 1)
            A.activation(act_dummy[:], zero[:], ACT.Gelu)

            def gelu(j, e):
                for ft in range(FT):
                    if ft % 4 == 0:
                        act.wait_ge(s["ex_h"], 2 * j + ft // 4 + 1)
                        act.wait_ge(s["ex_h_lo"], 2 * j + ft // 4 + 1)
                    last = A.activation(hid[:, ft * P:(ft + 1) * P], flat[:, 512 * H_BANK + ft * P:512 * H_BANK + (ft + 1) * P],
                                        ACT.Gelu, bias=b1T[:, bass.ds(e * FT + ft, 1)], scale=1.0 / (S_X * S_W))
                    if ft % 4 == 3:
                        last.then_inc(s["gelu_done"], 1)

            act.wait_ge(s["block_expert_ready"], 1)
            gelu(0, experts_of(A, 0)[0])
            with act.Fori(0, QUADS) as i:
                e = experts_of(A, i)
                for u in range(4):
                    gelu(4 * i + u + 1, e[u + 1])

        @block.vector
        def _(dve):
            V = nc.vector

            def row_stats(tag, t):
                return V.bn_stats(stats[:, t, :], acc[:, t, :]).then_inc(s["stats%s_done" % tag], 1)

            def row_scales(tag, eps):
                dve.wait_ge(s["stats%s_done" % tag], T)
                for t in range(T):
                    V.bn_aggr(meanvar[:, t, :], stats[:, t, :]).then_inc(s["meanvar%s_done" % tag], 1)
                dve.wait_ge(s["meanvar%s_done" % tag], T)
                V.tensor_scalar(std[:], meanvar[:, :, 1], eps, None, ALU.add).then_inc(s["var%s_done" % tag], 1)
                dve.wait_ge(s["std%s_done" % tag], 1)
                V.reciprocal(rstd[:], std[:]).then_inc(s["rstd%s_done" % tag], 1)
                dve.wait_ge(s["rstd%s_done" % tag], 1)

            def normalise(dst, t):
                return V.tensor_scalar(dst[:, t, :], acc[:, t, :], meanvar[:, t, 0:1], rstd[:, t:t + 1], ALU.subtract, ALU.mult)

            V.memset(acc[:, T - 1, :], 0.0).then_inc(s["x_tail_zero"], 1)
            dve.wait_ge(s["x_loaded"], 32)
            for t in range(T):
                row_stats("", t)
            row_scales("", EPS)
            for t in range(T):
                normalise(xn, t).then_inc(s["xn_ready"], 1)
            for k in range(TP + 1):
                w = 2 * P if k < TP else P
                dve.wait_ge(s["xT_hi"], k + 1)
                V.scalar_tensor_tensor(xnT[:, 1, :, 2 * P * k:2 * P * k + w], ps[:, k, 0:2 * w].rearrange("p (f n) -> p f n", f=DT),
                                       S_X, xnT[:, 0, :, 2 * P * k:2 * P * k + w], ALU.mult, ALU.subtract).then_inc(s["xT_lo"], 1)
            dve.wait_ge(s["b1_done"], 1)
            V.tensor_copy(b1T[:], ps[:, 6, 0:E * FT]).then_inc(s["b1_ready"], 1)
            V.memset(qT[:, :, :, PAD + N - 8:QW], 0.0).then_inc(s["pads_ready"], 1)
            V.memset(vT[:, :, :, PAD + N - 8:QW], 0.0).then_inc(s["pads_ready"], 1)
            def weights_lo(chunks):
                for c in chunks:
                    w = wqkv[c // 4][:, :, (c // 2) % 2, (c % 2) * 1024:(c % 2 + 1) * 1024]
                    dve.wait_ge(s["w_hi"], c + 1)
                    V.scalar_tensor_tensor(w[:, 1, :], stage[:, c % 3, :], S_W, w[:, 0, :], ALU.mult, ALU.subtract).then_inc(s["w_lo"], 1)

            def row_logits(h, t, c):
                i = h * T + t
                c0, w = CH[c]
                dve.wait_ge(s["qk_done"], 3 * i + c + 1)
                if c == 0:
                    dve.wait_ge(s["masks_ready"], t + 1)
                V.scalar_tensor_tensor(logits[:, c0:c0 + w], ps[:, S_BANK[c], 0:w], HALF / S_LOGIT,
                                       bias[:, bass.ds(t, 1), c0:c0 + w].rearrange("p t n -> p (t n)"),
                                       ALU.mult, ALU.add).then_inc(s["logits_done"], 1)

            def row_max(h, t, c):
                c0, w = CH[c]
                dve.wait_ge(s["logits_done"], 3 * (h * T + t) + c + 1)
                V.tensor_reduce(chunkmax[:, c:c + 1], logits[:, c0:c0 + w], AX.X, ALU.max).then_inc(s["chunkmax_done"], 1)

            def row_shift(h, t):
                i = h * T + t
                dve.wait_ge(s["chunkmax_done"], 3 * i + 3)
                V.tensor_reduce(col(rowmax, t), chunkmax[:, 0:3], AX.X, ALU.max).then_inc(s["rowmax_ready"], 1)
                dve.wait_ge(s["rowmax_ready"], i + 1)
                V.tensor_scalar(shift[:], col(rowmax, t), -1.0 / HALF, None, ALU.mult).then_inc(s["shift_ready"], 1)

            def probs_lo(i, g_):
                c0, k = PG[g_]
                dve.wait_ge(s["p_hi"], 3 * i + g_ + 1)
                V.scalar_tensor_tensor(probT[:, 1, c0 * P:(c0 + k) * P], ps[:, T_BANK + g_, 0:k * P], S_P,
                                       probT[:, 0, c0 * P:(c0 + k) * P], ALU.mult, ALU.subtract).then_inc(s["p_lo"], 1)

            def gather_rows(h, t):
                i = h * T + t
                V.reciprocal(recip[:], col(sums, t)).then_inc(s["recip_ready"], 1)
                dve.wait_ge(s["recip_ready"], i + 1)
                V.scalar_tensor_tensor(norm[:], col(rowmax, t), 0.5 * HALF * MASKED, recip[:], ALU.is_gt, ALU.mult).then_inc(s["norm_ready"], 1)
                dve.wait_ge(s["norm_ready"], i + 1)
                dve.wait_ge(s["av_done"], i + 1)
                V.scalar_tensor_tensor(sl(acc, t), ps[:, O_BANK, 0:D], norm[:], sl(acc, t), ALU.mult, ALU.add).then_inc(s["acc_done"], 1)

            def tile(h, t):
                i = h * T + t
                dve.wait_ge(s["exp_done"], i + 1)
                row_logits(h, t + 1, 0)
                row_max(h, t + 1, 0)
                row_logits(h, t + 1, 1)
                for g_ in range(3):
                    probs_lo(i, g_)
                row_max(h, t + 1, 1)
                row_logits(h, t + 1, 2)
                row_max(h, t + 1, 2)
                row_shift(h, t + 1)
                gather_rows(h, t)

            def head(h, first=False, last=False):
                _, c0 = head_start(h)
                for k in range(GROUPS):
                    if k == 4 and first:
                        weights_lo(range(8, 12))
                        dve.wait_ge(s["xn_ready"], T)
                        V.tensor_scalar(acc[:, :, :], acc[:, :, :], S_ACC, None, ALU.mult).then_inc(s["acc_done"], 1)
                    if k == 8:
                        dve.wait_ge(s["wo_hi"], h + 1)
                        V.scalar_tensor_tensor(wo_s[:, 1, :, :], wo_in, S_W, wo_s[:, 0, :, :], ALU.mult, ALU.subtract).then_inc(s["wo_free"], 1)
                    if k == 12:
                        for c in range(3):
                            row_logits(h, 0, c)
                            row_max(h, 0, c)
                        row_shift(h, 0)
                    dve.wait_ge(s["proj_hi"], GROUPS * h + k + 1)
                    hi, src, scale = group_io(k, 0, c0)
                    lo, _, _ = group_io(k, 1, c0)
                    V.scalar_tensor_tensor(lo, src, scale, hi, ALU.mult, ALU.subtract).then_inc(s["proj_lo"], 1)
                if last:
                    tile(h, 0)
                with dve.Fori(1 if last else 0, T - 1) as t:
                    tile(h, t)
                    if last:
                        V.bn_stats(sl(stats, t - 1), sl(acc, t - 1)).then_inc(s["stats2_done"], 1)
                for g_ in range(3):
                    probs_lo(h * T + T - 1, g_)
                gather_rows(h, T - 1)

            V.memset(dve_credit[:, 0:1], 0.0).then_inc(s["wo_free"], 1)
            weights_lo(range(8))
            head(0, first=True)
            with dve.Fori(1, H - 1) as h:
                head(h)
            head(H - 1, last=True)
            row_stats("2", T - 2)
            dve.wait_ge(s["gate_in"], 32)
            dve.wait_ge(s["wg_hi"], 1)
            V.scalar_tensor_tensor(wg_s[:, 1, :, :], wg_sb, S_W, wg_s[:, 0, :, :], ALU.mult, ALU.subtract).then_inc(s["wg_lo"], 1)
            dve.wait_ge(s["acc_done"], T * H + 1)
            row_stats("2", T - 1)
            row_scales("2", EPS * S_ACC * S_ACC)
            for t in range(T + 1):
                if t < T:
                    normalise(yn, t).then_inc(s["yn_ready"], 1)
                if t >= 1:
                    dve.wait_ge(s["ynsp_hi"], t)
                    V.scalar_tensor_tensor(ynsp[:, t - 1, 1, :], yn[:, t - 1, :], S_X, ynsp[:, t - 1, 0, :],
                                           ALU.mult, ALU.subtract).then_inc(s["ynsp_lo"], 1)
            dve.wait_ge(s["gate_done"], 1)
            V.scalar_tensor_tensor(glog, glog_ps, 1.0 / (S_X * S_W), bgbc.unsqueeze(1).to_broadcast([P, T, E]),
                                   ALU.mult, ALU.add).then_inc(s["glog_ready"], 1)
            dve.wait_ge(s["glog_ready"], 1)
            for t in range(T):
                V.max(top8[:, t, :], glog[:, t, :]).then_inc(s["top8_ready"], 1)
            dve.wait_ge(s["top8_ready"], T)
            V.tensor_tensor(gap, top8[:, :, 1], top8[:, :, 0], ALU.subtract).then_inc(s["gap_ready"], 1)
            for t in range(T):
                V.max_index(idx8[:, t, :], top8[:, t, :], glog[:, t, :]).then_inc(s["idx_ready"], 1)
            dve.wait_ge(s["idx_ready"], T)
            V.tensor_copy(idxf, idx8).then_inc(s["idxf_ready"], 1)
            dve.wait_ge(s["route_consts"], 8)
            dve.wait_ge(s["idxf_ready"], 1)
            for k, one in enumerate((one1, one2)):
                V.tensor_tensor(one, iota_f[:, 0:E].unsqueeze(1).to_broadcast([P, T, E]), idxf[:, :, k:k + 1].to_broadcast([P, T, E]),
                                ALU.is_equal).then_inc(s["onehot_ready"], 1)
            dve.wait_ge(s["onehot_ready"], 2)
            V.tensor_tensor(both, one1, one2, ALU.add).then_inc(s["chosen_sum"], 1)
            dve.wait_ge(s["chosen_sum"], 1)
            V.tensor_tensor(chosen[:, 0:T, :], both, rowok, ALU.mult).then_inc(s["chosen_ready"], 1)
            dve.wait_ge(s["expgap_ready"], 1)
            V.tensor_scalar(den, expgap, 1.0, None, ALU.add).then_inc(s["den_ready"], 1)
            dve.wait_ge(s["den_ready"], 1)
            V.reciprocal(gate[:, 0, :], den).then_inc(s["gate1_ready"], 1)
            dve.wait_ge(s["gate1_ready"], 1)
            V.tensor_tensor(gate[:, 1, :], expgap, gate[:, 0, :], ALU.mult).then_inc(s["gate2_ready"], 1)
            dve.wait_ge(s["rank_done"], 1)
            V.tensor_scalar(countsi, rank[:, T, :], float(P - 1), None, ALU.add).then_inc(s["countsi_ready"], 1)
            dve.wait_ge(s["countsi_ready"], 1)
            V.tensor_scalar(padi, countsi, -P, None, ALU.bitwise_and).then_inc(s["padi_ready"], 1)
            dve.wait_ge(s["padi_ready"], 1)
            V.tensor_copy(padf, padi).then_inc(s["padf_ready"], 1)
            dve.wait_ge(s["padf_ready"], 1)
            V.tensor_tensor_scan(ends, onesr, padf, 0.0, ALU.mult, ALU.add).then_inc(s["ends_ready"], 1)
            dve.wait_ge(s["ends_ready"], 1)
            V.tensor_tensor(base, ends, padf, ALU.subtract).then_inc(s["base_e_ready"], 1)
            dve.wait_ge(s["base_e_ready"], 1)
            V.tensor_tensor(slot_e, rank[:, 0:T, :], base.unsqueeze(1).to_broadcast([P, T, E]), ALU.add).then_inc(s["slot_e_ready"], 1)
            dve.wait_ge(s["slot_e_ready"], 1)
            for k, one in enumerate((one1, one2)):
                V.tensor_tensor(pick, one, slot_e, ALU.mult).then_inc(s["pick_ready"], 1)
                dve.wait_ge(s["pick_ready"], k + 1)
                V.tensor_reduce(slotf[:, k, :], pick, AX.X, ALU.add).then_inc(s["slotf_ready"], 1)
                dve.wait_ge(s["slotf_ready"], k + 1)
            V.tensor_copy(sloti, slotf).then_inc(s["sloti_ready"], 1)
            dve.wait_ge(s["sloti_ready"], 1)
            V.tensor_scalar(rowi, sloti, P - 1, None, ALU.bitwise_and).then_inc(s["rowi_ready"], 1)
            dve.wait_ge(s["rowi_ready"], 1)
            V.tensor_copy(rowf, rowi).then_inc(s["rowf_ready"], 1)
            dve.wait_ge(s["rowf_ready"], 1)
            V.tensor_tensor(blockf, slotf, rowf, ALU.subtract).then_inc(s["blockf_ready"], 1)
            dve.wait_ge(s["blockf_ready"], 1)
            for k in range(2):
                V.tensor_tensor(block_hot[:, k, :, :], jb_f.unsqueeze(1).to_broadcast([P, T, BLOCKS]),
                                blockf[:, k, :].unsqueeze(2).to_broadcast([P, T, BLOCKS]), ALU.is_equal).then_inc(s["block_hot_ready"], 1)
            for k in range(2):
                dve.wait_ge(s["block_hot_ready"], k + 1)
                V.tensor_tensor(block_id[:, k, :, :], block_hot[:, k, :, :],
                                ids[:, 0:T].unsqueeze(2).to_broadcast([P, T, BLOCKS]), ALU.mult).then_inc(s["block_id_ready"], 1)
                V.tensor_tensor(row_hot[:, k, :, :], iota_f.unsqueeze(1).to_broadcast([P, T, P]),
                                rowf[:, k, :].unsqueeze(2).to_broadcast([P, T, P]), ALU.is_equal).then_inc(s["row_hot_ready"], 1)
            V.tensor_tensor(jcmp[0:1, :, :], jb_f[0:1, :].unsqueeze(2).to_broadcast([1, BLOCKS, E]),
                            ends[0:1, :].unsqueeze(1).to_broadcast([1, BLOCKS, E]), ALU.is_ge).then_inc(s["jcmp_ready"], 1)
            dve.wait_ge(s["token_done"], 1)
            V.scalar_tensor_tensor(spare, token_ps, 0.0, ids[:, T:T + 1].to_broadcast([P, BLOCKS]), ALU.is_equal, ALU.mult
                                   ).then_inc(s["spare_ready"], 1)
            dve.wait_ge(s["spare_ready"], 1)
            V.scalar_tensor_tensor(token, token_ps, -1.0, spare, ALU.add, ALU.add).then_inc(s["token_ready"], 1)
            dve.wait_ge(s["jcmp_ready"], 1)
            V.tensor_reduce(jexp[0:1, :], jcmp[0:1, :, :], AX.X, ALU.add).then_inc(s["jexp_ready"], 1)
            dve.wait_ge(s["jexp_ready"], 1)
            V.tensor_scalar(jexp[0:1, :], jexp[0:1, :], float(E - 1), None, ALU.min).then_inc(s["jmin_ready"], 1)
            dve.wait_ge(s["jmin_ready"], 1)
            word = jexp[0:1, 4:BLOCKS:4]
            for u in range(3, -1, -1):
                dst = block_expert[0:1, :] if u == 0 else jword[0:1, :]
                V.scalar_tensor_tensor(dst, word, float(E), jexp[0:1, u:u + 4 * QUADS - 3:4], ALU.mult, ALU.add
                                       ).then_inc(s["block_expert_ready" if u == 0 else "jmin_ready"], 1)
                if u > 0:
                    dve.wait_ge(s["jmin_ready"], 5 - u)
                word = jword[0:1, :]
            dve.wait_ge(s["gate2_ready"], 1)
            V.tensor_tensor(gate, gate, rowok[:, :, 0].unsqueeze(1).to_broadcast([P, 2, T]), ALU.mult).then_inc(s["gate_ready"], 1)
            dve.wait_ge(s["gate_ready"], 1)
            V.tensor_scalar(gate_s[:, 0, :, :], gate, S_G, None, ALU.mult).then_inc(s["gate_hi"], 1)
            dve.wait_ge(s["gate_hi"], 1)
            V.scalar_tensor_tensor(gate_s[:, 1, :, :], gate, S_G, gate_s[:, 0, :, :], ALU.mult, ALU.subtract).then_inc(s["gate_lo"], 1)
            dve.wait_ge(s["gate_lo"], 1)
            for a in range(2):
                for k in range(2):
                    V.tensor_tensor(block_gate[:, a, k, :, :], block_hot[:, k, :, :],
                                    gate_s[:, a, k, :].unsqueeze(2).to_broadcast([P, T, BLOCKS]), ALU.mult).then_inc(s["block_gate_ready"], 1)
            V.scalar_tensor_tensor(acc[:, :, :], acc[:, :, :], 1.0 / S_ACC, yn, ALU.mult, ALU.add).then_inc(s["base_ready"], 1)
            dve.wait_ge(s["slot_gate_done"], 1)
            V.tensor_scalar(slot_gate, gate_ps, 1.0 / S_G, None, ALU.mult).then_inc(s["slot_gate_ready"], 1)
            dve.wait_ge(s["slot_gate_ready"], 1)

            def x_parts(j):
                dve.wait_ge(s["ex_T"], j + 1)
                V.tensor_copy(xT.rearrange("p s f n -> p (s f n)"), xt_bank).then_inc(s["ex_x"], 1)

            def h_parts(j):
                for half in range(2):
                    src = hid[:, 512 * half:512 * (half + 1)]
                    hi, lo = (hT[:, k, 4 * half:4 * half + 4, :].rearrange("p f n -> p (f n)") for k in range(2))
                    dve.wait_ge(s["gelu_done"], 2 * j + half + 1)
                    V.tensor_scalar(hi, src, S_H, None, ALU.mult).then_inc(s["ex_h_hi"], 1)
                    dve.wait_ge(s["ex_h_hi"], 2 * j + half + 1)
                    V.scalar_tensor_tensor(lo, src, S_H, hi, ALU.mult, ALU.subtract).then_inc(s["ex_h_lo"], 1)

            def y_rows(j, place, e, ring_used=True):
                if ring_used:
                    dve.wait_ge(s["mixed"], 16 * (j - YR + 1))
                dve.wait_ge(s["ex_o"], j + 1)
                V.scalar_tensor_tensor(yb[:, place, :], ps[:, Y_BANK, 0:D], 1.0 / (S_H * S_W), sl(b2bc, e),
                                       ALU.mult, ALU.add).then_inc(s["y_sum"], 1)
                dve.wait_ge(s["y_sum"], j + 1)
                V.tensor_scalar(yb[:, place, :], yb[:, place, :], col(slot_gate, j), None, ALU.mult).then_inc(s["ys_ready"], 1)

            def quad(i, first=False, last=False):
                e = experts_of(V, i)
                for u in range(4):
                    j = 4 * i + u + 1
                    if not (last and u == 3):
                        x_parts(j + 1)
                    y_rows(j - 1, u % YR, e[u], not first)
                    h_parts(j)
                if last:
                    y_rows(j, 4 % YR, e[4])

            V.memset(dve_credit[:, 1:2], 0.0).then_inc(s["ex_h_lo"], 2)
            dve.wait_ge(s["b2_loaded"], 16)
            dve.wait_ge(s["block_expert_ready"], 1)
            x_parts(0)
            x_parts(1)
            h_parts(0)
            quad(0, first=True)
            with dve.Fori(1, QUADS - 1) as i:
                quad(i)
            quad(QUADS - 1, last=True)

        @block.tensor
        def _(pe):
            M = nc.tensor

            def three(dst, lhs, rhs, start, stop):
                for n, (a, b) in enumerate(((0, 0), (0, 1), (1, 0))):
                    last = M.matmul(dst, lhs(a), rhs(b), start=start and n == 0, stop=stop and n == 2)
                return last

            def transposed(src, ready, done):
                for k in range(TP + 1):
                    tiles = 2 if k < TP else 1
                    for j in range(tiles):
                        pe.wait_ge(ready, 2 * k + j + 1)
                        for ft in range(DT):
                            last = M.transpose(ps[:, k, (ft * tiles + j) * P:(ft * tiles + j + 1) * P],
                                               src[:, 2 * k + j, ft * P:(ft + 1) * P], ident[:])
                    last.then_inc(done, 1)

            pe.wait_ge(s["consts_ready"], 3)
            transposed(xn, s["xn_ready"], s["xT_done"])
            pe.wait_ge(s["b1_loaded"], 16)
            M.transpose(ps[:, 6, 0:E * FT], b1rows, ident[0:E * FT, 0:E * FT]).then_inc(s["b1_done"], 1)

            def project(h, k, first=False):
                w, dst_dt, half = (wk_s, wq_s, wv_s)[k // 4], k // 2 % 2, k % 2
                t0, _ = head_start(h)
                if first and k % 4 == 0:
                    pe.wait_ge(s["w_lo"], k + 4)
                if k >= 4:
                    pe.wait_ge(s["proj_lo"], GROUPS * h + k - 3)
                elif not first and k < 2:
                    pe.wait_ge(s["logits_done"], 3 * T * h)
                elif not first:
                    pe.wait_ge(s["acc_done"], T * h + 1)
                dst = pair(k)
                for j in range(4):
                    b = 4 * half + j
                    for ft in range(DT):
                        last = three(dst[:, j, 0:WIN], lambda a: w[:, a, ft, b * D + dst_dt * P:b * D + (dst_dt + 1) * P],
                                     lambda c: xnT[:, c, ft, bass.ds(t0, WIN)], ft == 0, ft == DT - 1)
                last.then_inc(s["proj_done"], 1)

            def project_out(h, k):
                if k < 14:
                    pe.wait_ge(s["proj_lo"], GROUPS * h + 12)
                else:
                    pe.wait_ge(s["logits_done"], 3 * T * h + 3)
                dst = pair(k)
                c0, n = PG[k - 12]
                for j in range(n):
                    at = PAD + (c0 + j) * P
                    for ft in range(DT):
                        last = three(dst[:, j, 0:D], lambda a: vT[:, a, ft, at:at + P], lambda c: wo_s[:, c, ft, :],
                                     ft == 0, ft == DT - 1)
                last.then_inc(s["proj_done"], 1)

            def scores(h, t, c, first=False):
                c0, w = CH[c]
                if not first:
                    pe.wait_ge(s["logits_done"], 3 * (h * T + t) + c - 2)
                at = t * P + PAD
                for ft in range(DT):
                    last = three(ps[:, S_BANK[c], 0:w], lambda a: qT[:, a, ft, bass.ds(at, P)] if not first else qT[:, a, ft, PAD:PAD + P],
                                 lambda b: kT[:, b, ft, PAD + c0:PAD + c0 + w], ft == 0, ft == DT - 1)
                last.then_inc(s["qk_done"], 1)

            def transposes(h, t, g_):
                i = h * T + t
                if g_ == 0:
                    pe.wait_ge(s["exp_done"], i + 1)
                c0, n = PG[g_]
                for j in range(n):
                    last = M.transpose(ps[:, T_BANK + g_, j * P:(j + 1) * P], prob[:, (c0 + j) * P:(c0 + j + 1) * P], ident[:])
                last.then_inc(s["t_done"], 1)

            def attend(h, t):
                i = h * T + t
                pe.wait_ge(s["acc_done"], i + 1)
                for g_, (c0, n) in enumerate(PG):
                    pe.wait_ge(s["p_lo"], 3 * i + g_ + 1)
                    for c in range(c0, c0 + n):
                        k = P if c < T - 1 else TAIL
                        last = three(ps[:, O_BANK, 0:D], lambda a: probT[0:k, a, c * P:(c + 1) * P],
                                     lambda b: vo[0:k, b, c, :], c == 0, c == T - 1)
                last.then_inc(s["av_done"], 1)

            pe.wait_ge(s["xT_lo"], TP + 1)
            pe.wait_ge(s["b1_ready"], 1)
            pe.wait_ge(s["pads_ready"], 2)
            def head(h, first=False, last=False):
                for k in range(2, 12):
                    project(h, k, first)
                pe.wait_ge(s["proj_lo"], GROUPS * h + 10)
                for c in range(3):
                    scores(h, 0, c, first=True)
                pe.wait_ge(s["wo_free"], h + 2)
                for k in range(12, 15):
                    project_out(h, k)
                with pe.Fori(0, T - 1) as t:
                    scores(h, t + 1, 0)
                    scores(h, t + 1, 1)
                    pe.wait_ge(s["proj_lo"], GROUPS * h + GROUPS)
                    for g_ in range(3):
                        transposes(h, t, g_)
                    scores(h, t + 1, 2)
                    attend(h, t)
                if not last:
                    project(h + 1, 0)
                for g_ in range(3):
                    transposes(h, T - 1, g_)
                if not last:
                    project(h + 1, 1)
                attend(h, T - 1)

            project(0, 0, True)
            project(0, 1, True)
            head(0, first=True)
            with pe.Fori(1, H - 1) as h:
                head(h)
            head(H - 1, last=True)

            pe.wait_ge(s["acc_done"], T * H + 1)
            pe.wait_ge(s["wg_lo"], 1)
            for t in range(T + 1):
                if t < T:
                    pe.wait_ge(s["ynsp_lo"], t + 1)
                    if t >= 4:
                        pe.wait_ge(s["ynT_ready"], t - 3)
                    for q in range(2 * DT):
                        last = M.transpose(ynT_ps[t % 4][:, q * P:(q + 1) * P], ynsp[:, t, q // DT, (q % DT) * P:(q % DT + 1) * P], ident16[:])
                    last.then_inc(s["ynT_done"], 1)
                if t >= 1:
                    pe.wait_ge(s["ynT_ready"], t)
                    for ft in range(DT):
                        last = three(glog_ps[:, t - 1, :], lambda a: ynT[:, t - 1, a, ft, :], lambda b: wg_s[:, b, ft, :],
                                     ft == 0, ft == DT - 1)
            last.then_inc(s["gate_done"], 1)
            pe.wait_ge(s["route_consts"], 8)
            pe.wait_ge(s["chosen_ready"], 1)
            M.matmul(rank, ones, chosen[:, T:T + 1, :].to_broadcast([P, T + 1, E]), start=True, stop=False)
            for t in range(T):
                M.matmul(rank[:, t + 1:T + 1, :], ones, chosen[:, t:t + 1, :].to_broadcast([P, T - t, E]),
                         start=False, stop=False, skip_group_check=True)
            M.matmul(rank, tri, chosen, start=False, stop=True).then_inc(s["rank_done"], 1)
            for k in range(2):
                pe.wait_ge(s["row_hot_ready"], k + 1)
                pe.wait_ge(s["block_id_ready"], k + 1)
                for t in range(T):
                    last = M.matmul(token_ps, row_hot[:, k, t, :], block_id[:, k, t, :], start=k == 0 and t == 0, stop=k == 1 and t == T - 1)
            last.then_inc(s["token_done"], 1)
            pe.wait_ge(s["block_gate_ready"], 4)
            for k in range(2):
                for t in range(T):
                    for a in range(2):
                        last = M.matmul(gate_ps, row_hot[:, k, t, :], block_gate[:, a, k, t, :],
                                        start=k == 0 and t == 0 and a == 0, stop=k == 1 and t == T - 1 and a == 1)
            last.then_inc(s["slot_gate_done"], 1)

            def block_T(j, place, first=False):
                pe.wait_ge(s["x_in"], 16 * (j + 1))
                if not first:
                    pe.wait_ge(s["ex_x"], j)
                for q in range(2 * DT):
                    last = M.transpose(xt_bank[:, q * P:(q + 1) * P], xb[:, place, q * P:(q + 1) * P], ident16[:])
                last.then_inc(s["ex_T"], 1)

            def block_H(j, e, first=False):
                pe.wait_ge(s["experts_ready"], e + 1)
                pe.wait_ge(s["ex_x"], j + 1)
                for half in range(2):
                    if not first:
                        pe.wait_ge(s["gelu_done"], 2 * j - 1 + half)
                    for ft in range(4 * half, 4 * half + 4):
                        for k in range(DT):
                            last = three(flat[:, 512 * H_BANK + ft * P:512 * H_BANK + (ft + 1) * P],
                                         lambda a: w1_s[a][:, bass.ds(e, 1), k, ft * P:(ft + 1) * P].rearrange("p e n -> p (e n)"),
                                         lambda b: xT[:, b, k, :], k == 0, k == DT - 1)
                    last.then_inc(s["ex_h"], 1)

            def block_O(j, e, first=False):
                if not first:
                    pe.wait_ge(s["ys_ready"], j)
                for ft in range(FT):
                    if ft % 4 == 0:
                        pe.wait_ge(s["ex_h_lo"], 2 * j + ft // 4 + 3)
                    last = three(ps[:, Y_BANK, 0:D], lambda a: hT[:, a, ft, :],
                                 lambda b: w2_s[b][:, bass.ds(e, 1), ft, :].rearrange("p e n -> p (e n)"), ft == 0, ft == FT - 1)
                last.then_inc(s["ex_o"], 1)

            def quad(i, first=False, last=False):
                e = experts_of(M, i)
                for u in range(4):
                    j = 4 * i + u + 1
                    block_H(j, e[u + 1])
                    if not (last and u == 3):
                        block_T(j + 1, (u + 2) % XR)
                    block_O(j - 1, e[u], first and u == 0)
                if last:
                    block_O(j, e[4])

            pe.wait_ge(s["block_expert_ready"], 1)
            block_T(0, 0, first=True)
            block_H(0, experts_of(M, 0)[0], first=True)
            block_T(1, 1)
            quad(0, first=True)
            with pe.Fori(1, QUADS - 1) as i:
                quad(i)
            quad(QUADS - 1, last=True)


_INS = ["x", "adj", "L0_gnn_Wq", "L0_gnn_Wk", "L0_gnn_Wv", "L0_gnn_Wout", "L0_ffn_Wg", "L0_ffn_bg",
        "L0_ffn_W1", "L0_ffn_b1", "L0_ffn_W2", "L0_ffn_b2"]


def kernel(**inputs):
    import numpy as _np
    import concourse.bacc as _bacc
    from concourse import mybir as _mybir
    from concourse.bass_utils import run_bass_kernel_spmd as _run

    nc = _bacc.Bacc("TRN2", target_bir_lowering=False, num_devices=1)
    arrays, args = {}, []
    for name in _INS:
        a = _np.ascontiguousarray(inputs[name])
        arrays[f"in_{name}_dram"] = a
        args.append(nc.dram_tensor(f"in_{name}_dram", a.shape, _mybir.dt.from_np(a.dtype), kind="ExternalInput").ap())
    args.append(nc.dram_tensor("out_0_dram", (N, D), F32, kind="ExternalOutput").ap())
    args.append(nc.dram_tensor("w_split_dram", (E * P, 4, 2048), F16, kind="Internal").ap())
    args.append(nc.dram_tensor("yn_rows_dram", (N + P, 2 * D), F16, kind="Internal").ap())
    args.append(nc.dram_tensor("mix_dram", (N + P, D), F32, kind="Internal").ap())
    build(nc, *args)
    r = _run(nc, [arrays], core_ids=[0])
    return r.results[0]["out_0_dram"]
```

```python
from contextlib import ExitStack

import concourse.bass as bass
from concourse import mybir

ALU = mybir.AluOpType
ACT = mybir.ActivationFunctionType
AX = mybir.AxisListType
F32 = mybir.dt.float32
F16 = mybir.dt.float16
I32 = mybir.dt.int32
U32 = mybir.dt.uint32

P = 128
N = 1354
D = 256
H = 8
E = 8
FF = 1024
DT = D // P
FT = FF // P
T = (N + P - 1) // P
TAIL = N - (T - 1) * P
TP = T // 2
NP = T * P
BLOCKS = (2 * N + E * (P - 1)) // P
WIN = N // 8 + 2
PAD = 16
QW = PAD + NP
CH = [(0, 512), (512, 512), (1024, N - 1024)]
PG = [(0, 4), (4, 4), (8, T - 8)]
XR, YR = 4, 4
QUADS = (BLOCKS - 1) // 4
GROUPS = 15
EPS = 1e-5

S_X = 2.0 ** 8
S_W = 2.0 ** 9
S_Q = 2.0 ** 5
S_V = 2.0 ** 8
S_P = 2.0 ** 12
S_H = 2.0 ** 6
S_LOGIT = S_Q * S_Q * 16.0
HALF = 0.5
S_ACC = S_P * S_V
S_G = 2.0 ** 10
assert BLOCKS == 4 * QUADS + 1
MASKED = -1.0e6


class Map:

    def __init__(self, arena):
        self.arena, self.at = arena, 0

    def take(self, cols, dt):
        size = 4 if dt in (F32, I32, U32) else 2
        view = self.arena[:, self.at // 2:(self.at + cols * size) // 2]
        self.at += cols * size
        return view if dt == F16 else view.bitcast(dt)


def build(nc, x, adj, Wq, Wk, Wv, Wout, Wg, bg, W1, b1, W2, b2, out, w_split, yn_rows):
    with ExitStack() as ctx:
        def sb(name, shape, dt):
            return ctx.enter_context(nc.sbuf_tensor(name, shape, dt))

        def sem(name):
            return ctx.enter_context(nc.semaphore(name))

        ARENA = 198528 // 2
        arena = sb("arena", [P, ARENA], F16)
        acc = sb("acc", [P, T, D], F32)
        ident = sb("ident", [P, P], F32)
        ident16 = sb("ident16", [P, P], F16)
        wscale = sb("wscale", [P, 1], F32)
        zero = sb("zero", [P, 1], F32)
        b1T = sb("b1T", [P, E * FT], F32)
        sums = sb("sums", [P, T], F32)
        rowmax = sb("rowmax", [P, T], F32)
        chunkmax = sb("chunkmax", [P, 3], F32)
        pool_credit = sb("pool_credit", [P, 1], F32)
        dve_credit = sb("dve_credit", [P, 2], F32)
        shift = sb("shift", [P, 1], F32)
        act_dummy = sb("act_dummy", [P, 3], F32)
        recip = sb("recip", [P, 1], F32)
        norm = sb("norm", [P, 1], F32)
        stats = sb("stats", [P, T, 6], F32)
        meanvar = sb("meanvar", [P, T, 2], F32)
        std = sb("std", [P, T], F32)
        rstd = sb("rstd", [P, T], F32)

        m = Map(arena)
        wqkv = [m.take(2 * DT * H * D, F16).rearrange("p (s f n) -> p s f n", s=2, f=DT) for _ in range(3)]
        wk_s, wq_s, wv_s = wqkv
        xnT = m.take(2 * DT * NP, F16).rearrange("p (s f n) -> p s f n", s=2, f=DT)
        vT = m.take(2 * DT * QW, F16).rearrange("p (s f n) -> p s f n", s=2, f=DT)
        kT = m.take(2 * DT * QW, F16).rearrange("p (s f n) -> p s f n", s=2, f=DT)
        at_q = m.at
        qT = m.take(2 * DT * QW, F16).rearrange("p (s f n) -> p s f n", s=2, f=DT)
        m2 = Map(arena)
        m2.at = at_q
        xn = m2.take(T * D, F32).rearrange("p (t d) -> p t d", d=D)
        vo = m.take(2 * T * D, F16).rearrange("p (s t d) -> p s t d", s=2, d=D)
        wo_s = m.take(2 * DT * D, F16).rearrange("p (s f n) -> p s f n", s=2, f=DT)
        wo_in = m.take(DT * D, F32).rearrange("p (f n) -> p f n", f=DT)
        at_bias = m.at
        bias = m.take(T * N, F32).rearrange("p (t n) -> p t n", n=N)
        logits = m.take(N, F32)
        prob = m.take(NP, F32)
        probT = m.take(2 * NP, F16).rearrange("p (s n) -> p s n", s=2)
        at_stage = m.at
        stage = m.take(3 * 1024, F32).rearrange("p (s n) -> p s n", s=3)
        assert m.at <= 2 * ARENA, m.at
        split_out = stage[:, 2, :].bitcast(F16).rearrange("p (s n) -> p s n", s=2)
        b1rows = logits[0:E * FT, 0:P]
        ROOM = 9
        late = T - -(-ROOM * 1024 // N)
        w_room = bias[:, late:T, :].rearrange("p t n -> p (t n)")
        w_in = [w_room[:, 1024 * c:1024 * (c + 1)] for c in range(ROOM)] + [stage[:, c, :] for c in range(3)]
        POOL_CHUNK = 2

        def w_split_part(c, part):
            return wqkv[c // 4][:, part, c // 2 % 2, (c % 2) * 1024:(c % 2 + 1) * 1024]

        DVE_TILE = late - 1
        masked = stage[:, 0:2, :].rearrange("p s n -> p (s n)")[:, 0:N]

        f = Map(arena)
        we = f.take(E * 8192, F16).rearrange("p (e n) -> p e n", e=E)
        we_end = f.at
        w1_s = [we[:, :, 2048 * s:2048 * (s + 1)].rearrange("p e (f n) -> p e f n", f=DT) for s in range(2)]
        w2_s = [we[:, :, 4096 + 2048 * s:4096 + 2048 * (s + 1)].rearrange("p e (f n) -> p e f n", f=FT)
                for s in range(2)]
        f_x = f.take(T * 2 * D, F16)
        ynT = f_x.rearrange("p (t s f n) -> p t s f n", t=T, s=2, f=DT)
        xb = f_x[:, 0:XR * 2 * D].rearrange("p (j n) -> p j n", j=XR)
        yb = f_x[:, XR * 2 * D:(XR + YR) * 2 * D].bitcast(F32).rearrange("p (j d) -> p j d", j=YR)
        yn = f.take(T * D, F32).rearrange("p (t d) -> p t d", d=D)
        ynsp = f.take(T * 2 * D, F16).rearrange("p (t s d) -> p t s d", s=2, d=D)
        b2bc = f.take(E * D, F32).rearrange("p (e d) -> p e d", d=D)
        hid = f.take(FF, F32)
        hT = f.take(2 * FF, F16).rearrange("p (s f n) -> p s f n", s=2, f=FT)
        xT = f.take(2 * D, F16).rearrange("p (s f n) -> p s f n", s=2, f=DT)
        w1_lo = yn.rearrange("p t d -> p (t d)").bitcast(F16)[:, 0:2 * 2048].rearrange("p (j f n) -> p j f n", j=2, f=DT)
        row_hot = ynsp.rearrange("p t s d -> p (t s d)")[:, 0:2 * T * P].rearrange("p (k t n) -> p k t n", k=2, t=T)
        block_hot = f.take(2 * T * BLOCKS, F16).rearrange("p (k t j) -> p k t j", k=2, t=T)
        block_id = f.take(2 * T * BLOCKS, F16).rearrange("p (k t j) -> p k t j", k=2, t=T)
        f.at = max(f.at, at_stage)
        wg_sb = f.take(DT * E, F32).rearrange("p (f e) -> p f e", f=DT)
        wg_s = f.take(2 * DT * E, F16).rearrange("p (s f e) -> p s f e", s=2, f=DT)
        bgbc = f.take(E, F32)
        rowok = f.take(T * E, F32).rearrange("p (t e) -> p t e", e=E)
        chosen = f.take((T + 1) * E, F16).rearrange("p (t e) -> p t e", e=E)
        tri = f.take(P, F16)
        ones = f.take(P, F16)
        onesr = f.take(E, F32)
        iota_i = f.take(P, I32)
        iota_f = f.take(P, F16)
        jb_i = f.take(BLOCKS + 1, I32)
        jb_f = f.take(BLOCKS + 1, F16)
        ids_i = f.take(T + 1, I32)
        ids = f.take(T + 1, F16)
        glog = f.take(T * E, F32).rearrange("p (t e) -> p t e", e=E)
        top8 = f.take(T * E, F32).rearrange("p (t e) -> p t e", e=E)
        idx8 = f.take(T * E, U32).rearrange("p (t e) -> p t e", e=E)
        idxf = f.take(T * E, F16).rearrange("p (t e) -> p t e", e=E)
        one = f.take(2 * T * E, F32).rearrange("p (k t e) -> p k t e", k=2, e=E)
        slot_e = f.take(T * E, F32).rearrange("p (t e) -> p t e", e=E)
        pick = f.take(2 * T * E, F32).rearrange("p (k t e) -> p k t e", k=2, e=E)
        slotf = f.take(2 * T, F32).rearrange("p (k t) -> p k t", k=2)
        sloti = f.take(2 * T, I32).rearrange("p (k t) -> p k t", k=2)
        rowi = f.take(2 * T, I32).rearrange("p (k t) -> p k t", k=2)
        rowf = f.take(2 * T, F32).rearrange("p (k t) -> p k t", k=2)
        blockf = f.take(2 * T, F16).rearrange("p (k t) -> p k t", k=2)
        gate = f.take(2 * T, F32).rearrange("p (k t) -> p k t", k=2)
        gate_s = f.take(2 * 2 * T, F16).rearrange("p (s k t) -> p s k t", s=2, k=2)
        gap = f.take(T, F32)
        expgap = f.take(T, F32)
        den = f.take(T, F32)
        countsi = f.take(E, I32)
        padi = f.take(E, I32)
        padf = f.take(E, F32)
        ends = f.take(E, F32)
        base = f.take(E, F32)
        block_gate = f.take(2 * 2 * T * BLOCKS, F16).rearrange("p (s k t j) -> p s k t j", s=2, k=2, t=T)
        spare = f.take(BLOCKS, F32)
        token = f.take(BLOCKS, U32)
        slot_gate = f.take(BLOCKS, F32)
        jcmp = f.take((BLOCKS + 1) * E, F32).rearrange("p (j e) -> p j e", e=E)
        jexp = f.take(BLOCKS + 1, F32)
        jword = f.take(QUADS, F32)
        block_expert = f.take(QUADS, I32)
        assert f.at <= 2 * ARENA, f.at

        ps = ctx.enter_context(nc.psum_tensor("ps", [P, 8, 512], F32))
        flat = ps[:, :, :].rearrange("p b n -> p (b n)")
        S_BANK = (6, 7, 5)
        T_BANK, O_BANK = 1, 0
        xt_bank = ps[:, 0, 0:D].bitcast(F16)
        ynT_ps = [ps[:, b, 0:D].bitcast(F16) for b in (4, 5, 1, 2)]
        H_BANK, Y_BANK = 1, 3
        glog_ps = ps[:, 6, 0:T * E].rearrange("p (t e) -> p t e", e=E)
        rank = ps[:, 7, 0:(T + 1) * E].rearrange("p (t e) -> p t e", e=E)
        token_ps, gate_ps = ps[:, 4, 0:BLOCKS], ps[:, 5, 0:BLOCKS]

        names = """consts_ready x_tail_zero x_loaded0 x_loaded b1_loaded stats_done meanvar_done var_done std_done rstd_done
            xn_ready xT_done xT_hi xT_lo b1_done b1_ready w_hi w_lo w_scaled w_lo_pool
            masks_made masks_ready mask_dve_made mask_dve_ready pads_ready prob_pad
            wo_free wo_loaded wo_hi proj_done proj_hi proj_lo
            qk_done logits_done chunkmax_done rowmax_ready shift_ready exp_done t_done p_hi p_lo av_done recip_ready norm_ready acc_done
            stage_free piece_loaded0 piece_loaded1 piece_hi piece_scaled piece_stored
            stats2_done meanvar2_done var2_done std2_done rstd2_done yn_ready ynsp_hi ynsp_lo ynT_done ynT_ready
            gate_in wg_hi wg_lo gate_done glog_ready top8_ready idx_ready idxf_ready gap_ready expgap_ready den_ready gate1_ready
            gate2_ready gate_ready onehot_ready chosen_ready rank_done countsi_ready padi_ready padf_ready ends_ready
            base_e_ready slot_e_ready pick_ready slotf_ready sloti_ready rowi_ready rowf_ready blockf_ready
            row_hot_ready block_hot_ready block_id_ready token_done spare_ready token_ready
            gate_hi gate_lo block_gate_ready slot_gate_done slot_gate_ready
            jcmp_ready jexp_ready jmin_ready block_expert_ready route_ints route_consts
            base_ready yn_stored base_stored b2_loaded experts_ready x_in ex_T ex_x ex_w ex_h gelu_done ex_h_hi ex_h_lo ex_o
            y_sum ys_ready mixed""".split()
        s = {n: sem(n) for n in names}
        w_loaded = [sem(f"w_loaded{c}") for c in range(12)]
        expert_loaded = [sem(f"expert_loaded{e}") for e in range(E)]

        def head_start(h):
            return 169 * h + h // 4, PAD - (2 * h - 8 * (h // 4))

        assert N // 8 == 169 and N % 8 == 2
        PAIR = (4, 6, 2, 0) * 3 + (2, 0, 4)

        def pair(k):
            b = PAIR[k]
            return ps[:, b:b + 2, :].rearrange("p b (j n) -> p (b j) n", j=2)

        def group_io(k, part, c0):
            if k >= 12:
                a, n = PG[k - 12]
                return vo[:, part, a:a + n, :], pair(k)[:, 0:n, :], S_V / (S_Q * S_W)
            buf, q = (kT, qT, vT)[k // 4], k % 4
            rows = buf[:, part, q // 2, bass.ds(c0, 8 * WIN)].rearrange("p (t b) -> p b t", b=8)
            return rows[:, 4 * (q % 2):4 * (q % 2) + 4, :], pair(k)[:, :, 0:WIN], S_Q / (S_X * S_W)

        def col(buf, t):
            return buf[:, bass.ds(t, 1)]

        def sl(buf, t):
            return buf[:, bass.ds(t, 1), :].rearrange("p t n -> p (t n)")

        W1r = W1.rearrange("e k n -> (e k) n")
        W2r = W2.rearrange("e k n -> (e k) n")
        ADJ = [(0, 1), (1, late), (late, T - 1), (T - 1, T)]
        adj_in = [sem(f"adj_in{k}") for k in range(len(ADJ))]

        def experts_of(eng, i, n=5):
            word = eng.value_load(block_expert[0:1, bass.ds(i, 1)], min_val=0, max_val=E ** 6 - 1)
            return [eng.snap((word // E ** u) % E, min_val=0, max_val=E - 1) for u in range(n)]

        def token_rows(dram, view):
            left = N + P - NP
            return ((dram[0:NP, :].rearrange("(t p) d -> p t d", p=P), view), (dram[NP:N + P, :], view[0:left, 0, :]))

        block = ctx.enter_context(nc.Block())

        @block.sync
        def _(sp):
            sp.wait_ge(s["x_tail_zero"], 1)
            sp.dma_start(acc[:, 0:TP, :], x[0:TP * P, :].rearrange("(t p) d -> p t d", p=P)).then_inc(s["x_loaded0"], 16)
            sp.dma_start(acc[:, TP:T - 1, :], x[TP * P:(T - 1) * P, :].rearrange("(t p) d -> p t d", p=P)).then_inc(s["x_loaded"], 16)
            sp.dma_start(acc[0:TAIL, T - 1, :], x[(T - 1) * P:N, :]).then_inc(s["x_loaded"], 16)
            sp.dma_start(b1rows, b1.rearrange("e (f p) -> (e f) p", p=P)).then_inc(s["b1_loaded"], 16)
            for c in range(12):
                w, ft, half = (Wk, Wq, Wv)[c // 4], c // 2 % 2, c % 2
                sp.dma_start(w_in[c], w[ft * P:(ft + 1) * P, half * 1024:(half + 1) * 1024]).then_inc(w_loaded[c], 16)

            def wout(h):
                sp.wait_ge(s["wo_free"], h + 1)
                sp.dma_start(wo_in, Wout[bass.ds(h * D, D), :].rearrange("(f p) n -> p f n", p=P)).then_inc(s["wo_loaded"], 16)

            def expert_weights(e):
                for q in range(4):
                    sp.wait_ge(s["stage_free"], e * 4 + q + 1)
                    if q < 2:
                        src = W1r[bass.ds(e * D + q * P, P), :]
                        dst = stage[:, q % 2, :]
                    else:
                        src = W2r[bass.ds(e * FF + (q - 2) * 512, 512), :].rearrange("(f p) n -> p f n", p=P)
                        dst = stage[:, q % 2, :].rearrange("p (f n) -> p f n", n=D)
                    sp.dma_start(dst, src).then_inc(s[f"piece_loaded{q % 2}"], 16)

            wout(0)
            for k, (a, b) in enumerate(ADJ[0:3]):
                if k == 2:
                    sp.wait_ge(s["w_lo"], ROOM - 1)
                sp.dma_start(bias[:, a:b, :], adj[a * P:b * P, :].rearrange("(t p) n -> p t n", p=P)).then_inc(adj_in[k], 16)
            sp.wait_ge(s["masks_made"], 1)
            sp.dma_start(bias[0:TAIL, T - 1, :], adj[(T - 1) * P:N, :]).then_inc(adj_in[3], 16)
            expert_weights(0)
            with sp.Fori(1, H) as h:
                wout(h)
                expert_weights(h)
            sp.wait_ge(s["piece_stored"], 16 * 4 * E)
            sp.dma_start(wg_sb, Wg.rearrange("(f p) e -> p f e", p=P)).then_inc(s["gate_in"], 16)
            sp.dma_start(bgbc, bg.partition_broadcast(P)).then_inc(s["gate_in"], 16)

            def expert_in(e):
                sp.dma_start(we[:, e, :].rearrange("p (k n) -> p k n", k=4), w_split[e * P:(e + 1) * P, :, :]).then_inc(expert_loaded[e], 16)

            def experts_in(es):
                for e in es:
                    sp.wait_ge(expert_loaded[e], 16)
                    sp.sem_inc(s["experts_ready"], 1)

            sp.wait_ge(s["proj_done"], GROUPS * H)
            for e in range(4):
                expert_in(e)
            experts_in(range(4))
            used = -(-(we_end - at_bias) // (4 * N))
            sp.wait_ge(s["logits_done"], 3 * (T * (H - 1) + used))
            expert_in(7)
            sp.wait_ge(s["qk_done"], 3 * T * H)
            expert_in(4)
            sp.wait_ge(s["ynsp_lo"], T)
            for rows, view in token_rows(yn_rows, ynsp.rearrange("p t s d -> p t (s d)")):
                sp.dma_start(rows, view).then_inc(s["yn_stored"], 16)
            sp.wait_ge(s["acc_done"], T * H + 1)
            sp.dma_start(b2bc, b2.partition_broadcast(P)).then_inc(s["b2_loaded"], 16)
            expert_in(5)
            sp.wait_ge(s["base_ready"], 1)
            for rows, view in token_rows(out, acc[:, :, :]):
                sp.dma_start(rows, view).then_inc(s["base_stored"], 16)
            sp.wait_ge(s["x_in"], 16 * (XR + 1))
            expert_in(6)
            experts_in(range(4, E))
            sp.wait_ge(s["mixed"], 16 * BLOCKS)

        @block.gpsimd
        def _(pool):
            gp = nc.gpsimd
            gp.memset(ident[:], 0.0).then_inc(s["consts_ready"], 1)
            pool.wait_ge(s["consts_ready"], 1)
            gp.affine_select(out=ident[:], in_=ident[:], compare_op=ALU.not_equal, fill=1.0, base=0,
                             pattern=[[-1, P]], channel_multiplier=1).then_inc(s["consts_ready"], 1)
            pool.wait_ge(s["consts_ready"], 2)
            gp.tensor_scalar(ident16[:], ident[:], 1.0, None, ALU.mult).then_inc(s["consts_ready"], 1)
            gp.memset(wscale[:], S_W).then_inc(s["consts_ready"], 1)
            gp.memset(zero[:], 0.0).then_inc(s["consts_ready"], 1)
            gp.memset(prob[:, N:NP], 0.0).then_inc(s["prob_pad"], 1)
            pool.wait_ge(s["consts_ready"], 5)
            pool.wait_ge(s["w_hi"], POOL_CHUNK + 1)
            gp.tensor_tensor(w_in[POOL_CHUNK], w_in[POOL_CHUNK], wscale[:].to_broadcast([P, 1024]), ALU.mult).then_inc(s["w_scaled"], 1)
            pool.wait_ge(s["w_scaled"], 1)
            gp.tensor_tensor(w_split_part(POOL_CHUNK, 1), w_in[POOL_CHUNK], w_split_part(POOL_CHUNK, 0), ALU.subtract).then_inc(s["w_lo_pool"], 1)
            pool.wait_ge(s["w_lo"], ROOM - 1)
            gp.memset(bias[:, T - 1, :], 0.0).then_inc(s["masks_made"], 1)
            pool.wait_ge(s["w_lo"], 11)
            for k, (a, b) in enumerate(ADJ):
                pool.wait_ge(adj_in[k], 16)
                for t in range(a, b):
                    if t == DVE_TILE:
                        pool.wait_ge(s["mask_dve_ready"], 1)
                        gp.sem_inc(s["masks_ready"], 1)
                        continue
                    row = bias[:, t, :]
                    gp.tensor_scalar(masked, row, 0.0, HALF * MASKED, ALU.is_equal, ALU.mult).then_inc(s["masks_made"], 1)
                    pool.wait_ge(s["masks_made"], t + 2 - (t > DVE_TILE))
                    gp.tensor_tensor(row, row, masked, ALU.add).then_inc(s["masks_ready"], 1)
                    pool.wait_ge(s["masks_ready"], t + 1)
            pool.wait_ge(s["consts_ready"], 5)
            gp.memset(pool_credit[:], 0.0).then_inc(s["stage_free"], 2)
            with pool.Fori(0, E) as e:
                for q in range(4):
                    n = e * 4 + q
                    src = stage[:, q % 2, :]
                    pool.wait_ge(s[f"piece_loaded{q % 2}"], 32 * e + 16 * (q // 2) + 16)
                    gp.tensor_tensor(src, src, wscale[:].to_broadcast([P, 1024]), ALU.mult).then_inc(s["piece_scaled"], 1)
                    pool.wait_ge(s["piece_scaled"], n + 1)
                    gp.tensor_tensor(split_out[:, 0, :], src, zero[:].to_broadcast([P, 1024]), ALU.add).then_inc(s["piece_hi"], 1)
                    pool.wait_ge(s["piece_hi"], n + 1)
                    gp.tensor_tensor(split_out[:, 1, :], src, split_out[:, 0, :], ALU.subtract).then_inc(s["stage_free"], 1)
                    pool.wait_ge(s["stage_free"], n + 3)
                    a, c = 2 * (q // 2), (q % 2) * 1024
                    dst = w_split[bass.ds(e * P, P), a:a + 2, c:c + 1024]
                    gp.dma_start(dst, split_out).then_inc(s["piece_stored"], 16)
                    pool.wait_ge(s["piece_stored"], 16 * n + 16)
            pool.wait_ge(s["piece_stored"], 16 * 4 * E)
            gp.iota(iota_i, pattern=[[1, P]], base=0, channel_multiplier=0).then_inc(s["route_ints"], 1)
            gp.iota(jb_i, pattern=[[P, BLOCKS + 1]], base=0, channel_multiplier=0).then_inc(s["route_ints"], 1)
            gp.iota(ids_i[:, 0:T], pattern=[[P, T]], base=1, channel_multiplier=1).then_inc(s["route_ints"], 1)
            gp.iota(ids_i[:, T:T + 1], pattern=[[1, 1]], base=N + 1, channel_multiplier=1).then_inc(s["route_ints"], 1)
            gp.memset(chosen, 0.0).then_inc(s["route_ints"], 1)
            gp.memset(rowok, 1.0).then_inc(s["route_ints"], 1)
            gp.memset(tri, 1.0).then_inc(s["route_ints"], 1)
            gp.memset(ones, 1.0).then_inc(s["route_consts"], 1)
            gp.memset(onesr, 1.0).then_inc(s["route_consts"], 1)
            pool.wait_ge(s["route_ints"], 7)
            gp.tensor_scalar(iota_f, iota_i, 1.0, None, ALU.mult).then_inc(s["route_consts"], 1)
            gp.tensor_scalar(jb_f, jb_i, 1.0, None, ALU.mult).then_inc(s["route_consts"], 1)
            gp.tensor_scalar(ids, ids_i, 1.0, None, ALU.mult).then_inc(s["route_consts"], 1)
            gp.affine_select(out=rowok, in_=rowok, compare_op=ALU.is_ge, fill=0.0, base=N - 1,
                             pattern=[[-P, T], [0, E]], channel_multiplier=-1).then_inc(s["route_consts"], 1)
            gp.affine_select(out=tri, in_=tri, compare_op=ALU.is_ge, fill=0.0, base=-1,
                             pattern=[[1, P]], channel_multiplier=-1).then_inc(s["route_consts"], 1)
            pool.wait_ge(s["route_consts"], 7)
            gp.tensor_tensor(ids[:, 0:T], ids[:, 0:T], rowok[:, :, 0], ALU.mult).then_inc(s["route_consts"], 1)
            for k in range(2):
                pool.wait_ge(s["block_hot_ready"], k + 1)
                gp.tensor_tensor(block_id[:, k, :, :], block_hot[:, k, :, :],
                                 ids[:, 0:T].unsqueeze(2).to_broadcast([P, T, BLOCKS]), ALU.mult).then_inc(s["block_id_ready"], 1)

            def gather(j):
                gp.indirect_dma_start(xb[:, j % XR, :], None, yn_rows[:, :],
                                      bass.IndirectOffsetOnAxis(ap=token[:, j:j + 1], axis=0)).then_inc(s["x_in"], 16)

            pool.wait_ge(s["token_ready"], 1)
            pool.wait_ge(s["yn_stored"], 32)
            pool.wait_ge(s["gate_done"], 1)
            for j in range(XR):
                if j > 0:
                    pool.wait_ge(s["x_in"], 16 * j)
                gather(j)
            for j in range(BLOCKS):
                if j + XR < BLOCKS:
                    pool.wait_ge(s["ex_T"], j + 1)
                    pool.wait_ge(s["x_in"], 16 * (j + XR))
                    gather(j + XR)
                pool.wait_ge(s["ys_ready"], j + 1)
                if j == 0:
                    pool.wait_ge(s["base_stored"], 32)
                else:
                    pool.wait_ge(s["mixed"], 16 * j)
                gp.indirect_dma_start(out[:, :], bass.IndirectOffsetOnAxis(ap=token[:, j:j + 1], axis=0), yb[:, j % YR, :], None,
                                      compute_op=ALU.add).then_inc(s["mixed"], 16)

        @block.scalar
        def _(act):
            A = nc.scalar

            def copy(dst, src, scale):
                return A.activation(dst, src, ACT.Copy, scale=scale)

            def weights_hi(chunks):
                for c in chunks:
                    act.wait_ge(w_loaded[c], 16)
                    copy(w_split_part(c, 0), w_in[c], S_W).then_inc(s["w_hi"], 1)

            weights_hi(range(2))
            act.wait_ge(s["var_done"], 1)
            A.activation(std[:], std[:], ACT.Sqrt).then_inc(s["std_done"], 1)
            weights_hi(range(2, 4))
            for k in range(TP + 1):
                w = 2 * P if k < TP else P
                act.wait_ge(s["xT_done"], k + 1)
                copy(xnT[:, 0, :, 2 * P * k:2 * P * k + w], ps[:, k, 0:2 * w].rearrange("p (f n) -> p f n", f=DT), S_X
                     ).then_inc(s["xT_hi"], 1)
            def probs(h, t):
                i = h * T + t
                act.wait_ge(s["shift_ready"], i + 1)
                A.activation(prob[:, 0:N], logits, ACT.Exp, bias=shift[:], scale=1.0 / HALF,
                             accum_out=col(sums, t)).then_inc(s["exp_done"], 1)

            def probs_hi(i):
                for g_, (c0, k) in enumerate(PG):
                    act.wait_ge(s["t_done"], 3 * i + g_ + 1)
                    copy(probT[:, 0, c0 * P:(c0 + k) * P], ps[:, T_BANK + g_, 0:k * P], S_P).then_inc(s["p_hi"], 1)

            def head(h, first=False, last=False):
                _, c0 = head_start(h)
                for k in range(GROUPS):
                    if k == 4 and first:
                        weights_hi(range(8, 12))
                    if k == 8:
                        act.wait_ge(s["wo_loaded"], 16 * h + 16)
                        copy(wo_s[:, 0, :, :], wo_in, S_W).then_inc(s["wo_hi"], 1)
                    if k == 12:
                        probs(h, 0)
                    act.wait_ge(s["proj_done"], GROUPS * h + k + 1)
                    dst, src, scale = group_io(k, 0, c0)
                    copy(dst, src, scale).then_inc(s["proj_hi"], 1)
                with act.Fori(0, T - 1) as t:
                    i = h * T + t
                    probs_hi(i)
                    probs(h, t + 1)
                probs_hi(h * T + T - 1)
                if last:
                    act.wait_ge(s["var2_done"], 1)
                    A.activation(std[:, 0:T - 1], std[:, 0:T - 1], ACT.Sqrt).then_inc(s["std2_done"], 1)

            act.wait_ge(s["consts_ready"], 5)
            A.activation(act_dummy[:, 0:1], zero[:], ACT.Exp)
            weights_hi(range(4, 8))
            head(0, first=True)
            with act.Fori(1, H - 1) as h:
                head(h)
            act.wait_ge(s["gate_in"], 32)
            copy(wg_s[:, 0, :, :], wg_sb, S_W).then_inc(s["wg_hi"], 1)
            head(H - 1, last=True)
            for t in range(T + 2):
                if t == 5:
                    act.wait_ge(s["var2_done"], 2)
                    A.activation(std[:, T - 1:T], std[:, T - 1:T], ACT.Sqrt).then_inc(s["std2_done"], 1)
                if t < T:
                    act.wait_ge(s["yn_ready"], t + 1)
                    copy(ynsp[:, t, 0, :], yn[:, t, :], S_X).then_inc(s["ynsp_hi"], 1)
                if t >= 2:
                    act.wait_ge(s["ynT_done"], t - 1)
                    copy(ynT[:, t - 2, :, :, :].rearrange("p s f n -> p (s f n)"), ynT_ps[(t - 2) % 4], 1.0).then_inc(s["ynT_ready"], 1)
            A.activation(act_dummy[:, 1:2], zero[:], ACT.Exp)
            act.wait_ge(s["gap_ready"], 1)
            A.activation(expgap, gap, ACT.Exp).then_inc(s["expgap_ready"], 1)
            A.activation(act_dummy[:, 2:3], zero[:], ACT.Gelu)

            def gelu(j, e):
                for ft in range(FT):
                    if ft % 4 == 0:
                        act.wait_ge(s["ex_h"], 2 * j + ft // 4 + 1)
                        act.wait_ge(s["ex_h_lo"], 2 * j + ft // 4 + 1)
                    last = A.activation(hid[:, ft * P:(ft + 1) * P], flat[:, 512 * H_BANK + ft * P:512 * H_BANK + (ft + 1) * P],
                                        ACT.Gelu, bias=b1T[:, bass.ds(e * FT + ft, 1)], scale=1.0 / (S_X * S_W))
                    if ft % 4 == 3:
                        last.then_inc(s["gelu_done"], 1)

            act.wait_ge(s["block_expert_ready"], 1)
            gelu(0, experts_of(A, 0)[0])
            with act.Fori(0, QUADS) as i:
                e = experts_of(A, i)
                for u in range(4):
                    gelu(4 * i + u + 1, e[u + 1])

        @block.vector
        def _(dve):
            V = nc.vector

            def row_stats(tag, t):
                return V.bn_stats(stats[:, t, :], acc[:, t, :]).then_inc(s["stats%s_done" % tag], 1)

            def row_vars(tag, a, b, eps):
                dve.wait_ge(s["stats%s_done" % tag], b)
                for t in range(a, b):
                    V.bn_aggr(meanvar[:, t, :], stats[:, t, :]).then_inc(s["meanvar%s_done" % tag], 1)
                dve.wait_ge(s["meanvar%s_done" % tag], b)
                V.tensor_scalar(std[:, a:b], meanvar[:, a:b, 1], eps, None, ALU.add).then_inc(s["var%s_done" % tag], 1)

            def row_scales(tag, a, b, n):
                dve.wait_ge(s["std%s_done" % tag], n)
                V.reciprocal(rstd[:, a:b], std[:, a:b]).then_inc(s["rstd%s_done" % tag], 1)
                dve.wait_ge(s["rstd%s_done" % tag], n)

            def normalise(dst, t):
                return V.tensor_scalar(dst[:, t, :], acc[:, t, :], meanvar[:, t, 0:1], rstd[:, t:t + 1], ALU.subtract, ALU.mult)

            V.memset(acc[:, T - 1, :], 0.0).then_inc(s["x_tail_zero"], 1)
            for t in range(T):
                if t == 0:
                    dve.wait_ge(s["x_loaded0"], 16)
                if t == TP:
                    dve.wait_ge(s["x_loaded"], 32)
                row_stats("", t)
            row_vars("", 0, T, EPS)
            row_scales("", 0, T, 1)
            for t in range(T):
                normalise(xn, t).then_inc(s["xn_ready"], 1)
            for k in range(TP + 1):
                w = 2 * P if k < TP else P
                dve.wait_ge(s["xT_hi"], k + 1)
                V.scalar_tensor_tensor(xnT[:, 1, :, 2 * P * k:2 * P * k + w], ps[:, k, 0:2 * w].rearrange("p (f n) -> p f n", f=DT),
                                       S_X, xnT[:, 0, :, 2 * P * k:2 * P * k + w], ALU.mult, ALU.subtract).then_inc(s["xT_lo"], 1)
            def weights_lo(chunks):
                for c in chunks:
                    if c != POOL_CHUNK:
                        dve.wait_ge(s["w_hi"], c + 1)
                        V.scalar_tensor_tensor(w_split_part(c, 1), w_in[c], S_W, w_split_part(c, 0), ALU.mult, ALU.subtract
                                               ).then_inc(s["w_lo"], 1)

            def row_logits(h, t, c):
                i = h * T + t
                c0, w = CH[c]
                dve.wait_ge(s["qk_done"], 3 * i + c + 1)
                if c == 0:
                    dve.wait_ge(s["masks_ready"], t + 1)
                V.scalar_tensor_tensor(logits[:, c0:c0 + w], ps[:, S_BANK[c], 0:w], HALF / S_LOGIT,
                                       bias[:, bass.ds(t, 1), c0:c0 + w].rearrange("p t n -> p (t n)"),
                                       ALU.mult, ALU.add).then_inc(s["logits_done"], 1)

            def row_max(h, t, c):
                c0, w = CH[c]
                dve.wait_ge(s["logits_done"], 3 * (h * T + t) + c + 1)
                V.tensor_reduce(chunkmax[:, c:c + 1], logits[:, c0:c0 + w], AX.X, ALU.max).then_inc(s["chunkmax_done"], 1)

            def row_shift(h, t):
                i = h * T + t
                dve.wait_ge(s["chunkmax_done"], 3 * i + 3)
                V.tensor_reduce(col(rowmax, t), chunkmax[:, 0:3], AX.X, ALU.max).then_inc(s["rowmax_ready"], 1)
                dve.wait_ge(s["rowmax_ready"], i + 1)
                V.tensor_scalar(shift[:], col(rowmax, t), -1.0 / HALF, None, ALU.mult).then_inc(s["shift_ready"], 1)

            def probs_lo(i, g_):
                c0, k = PG[g_]
                dve.wait_ge(s["p_hi"], 3 * i + g_ + 1)
                V.scalar_tensor_tensor(probT[:, 1, c0 * P:(c0 + k) * P], ps[:, T_BANK + g_, 0:k * P], S_P,
                                       probT[:, 0, c0 * P:(c0 + k) * P], ALU.mult, ALU.subtract).then_inc(s["p_lo"], 1)

            def gather_rows(h, t):
                i = h * T + t
                V.reciprocal(recip[:], col(sums, t)).then_inc(s["recip_ready"], 1)
                dve.wait_ge(s["recip_ready"], i + 1)
                V.scalar_tensor_tensor(norm[:], col(rowmax, t), 0.5 * HALF * MASKED, recip[:], ALU.is_gt, ALU.mult).then_inc(s["norm_ready"], 1)
                dve.wait_ge(s["norm_ready"], i + 1)
                dve.wait_ge(s["av_done"], i + 1)
                V.scalar_tensor_tensor(sl(acc, t), ps[:, O_BANK, 0:D], norm[:], sl(acc, t), ALU.mult, ALU.add).then_inc(s["acc_done"], 1)

            def expert_inputs(t):
                if t < T:
                    normalise(yn, t).then_inc(s["yn_ready"], 1)
                if t >= 1:
                    dve.wait_ge(s["ynsp_hi"], t)
                    V.scalar_tensor_tensor(ynsp[:, t - 1, 1, :], yn[:, t - 1, :], S_X, ynsp[:, t - 1, 0, :],
                                           ALU.mult, ALU.subtract).then_inc(s["ynsp_lo"], 1)

            def tile(h, t):
                i = h * T + t
                dve.wait_ge(s["exp_done"], i + 1)
                row_logits(h, t + 1, 0)
                row_max(h, t + 1, 0)
                row_logits(h, t + 1, 1)
                for g_ in range(3):
                    probs_lo(i, g_)
                row_max(h, t + 1, 1)
                row_logits(h, t + 1, 2)
                row_max(h, t + 1, 2)
                row_shift(h, t + 1)
                gather_rows(h, t)

            def head(h, first=False, last=False):
                _, c0 = head_start(h)
                for k in range(GROUPS):
                    if k == 4 and first:
                        weights_lo(range(8, 12))
                    if k == 8:
                        dve.wait_ge(s["wo_hi"], h + 1)
                        V.scalar_tensor_tensor(wo_s[:, 1, :, :], wo_in, S_W, wo_s[:, 0, :, :], ALU.mult, ALU.subtract).then_inc(s["wo_free"], 1)
                    if k == 10 and first:
                        dve.wait_ge(s["xn_ready"], T)
                        V.tensor_scalar(acc[:, :, :], acc[:, :, :], S_ACC, None, ALU.mult).then_inc(s["acc_done"], 1)
                    if k == 12:
                        for c in range(3):
                            row_logits(h, 0, c)
                            row_max(h, 0, c)
                        row_shift(h, 0)
                        if first:
                            row, mask = bias[:, DVE_TILE, :], probT.rearrange("p s n -> p (s n)").bitcast(F32)[:, 0:N]
                            dve.wait_ge(adj_in[1], 16)
                            V.tensor_scalar(mask, row, 0.0, HALF * MASKED, ALU.is_equal, ALU.mult).then_inc(s["mask_dve_made"], 1)
                            dve.wait_ge(s["mask_dve_made"], 1)
                            V.tensor_tensor(row, row, mask, ALU.add).then_inc(s["mask_dve_ready"], 1)
                    dve.wait_ge(s["proj_hi"], GROUPS * h + k + 1)
                    hi, src, scale = group_io(k, 0, c0)
                    lo, _, _ = group_io(k, 1, c0)
                    V.scalar_tensor_tensor(lo, src, scale, hi, ALU.mult, ALU.subtract).then_inc(s["proj_lo"], 1)
                if last:
                    tile(h, 0)
                with dve.Fori(1 if last else 0, T - 1) as t:
                    tile(h, t)
                    if last:
                        V.bn_stats(sl(stats, t - 1), sl(acc, t - 1)).then_inc(s["stats2_done"], 1)
                if last:
                    dve.wait_ge(s["acc_done"], T * H)
                    row_stats("2", T - 2)
                    row_vars("2", 0, T - 1, EPS * S_ACC * S_ACC)
                    for g_ in range(3):
                        probs_lo(h * T + T - 1, g_)
                    row_scales("2", 0, T - 1, 1)
                    for t in range(5):
                        expert_inputs(t)
                    gather_rows(h, T - 1)
                    dve.wait_ge(s["acc_done"], T * H + 1)
                    row_stats("2", T - 1)
                    row_vars("2", T - 1, T, EPS * S_ACC * S_ACC)
                    for t in range(5, T - 1):
                        expert_inputs(t)
                    row_scales("2", T - 1, T, 2)
                    for t in range(T - 1, T + 1):
                        expert_inputs(t)
                else:
                    for g_ in range(3):
                        probs_lo(h * T + T - 1, g_)
                    gather_rows(h, T - 1)

            V.memset(dve_credit[:, 0:1], 0.0).then_inc(s["wo_free"], 1)
            weights_lo(range(4))
            dve.wait_ge(s["b1_done"], 1)
            V.tensor_copy(b1T[:], ps[:, 6, 0:E * FT]).then_inc(s["b1_ready"], 1)
            V.memset(qT[:, :, :, PAD + N - 8:QW], 0.0).then_inc(s["pads_ready"], 1)
            V.memset(vT[:, :, :, PAD + N - 8:QW], 0.0).then_inc(s["pads_ready"], 1)
            weights_lo(range(4, 8))
            head(0, first=True)
            with dve.Fori(1, H - 1) as h:
                head(h)
            dve.wait_ge(s["gate_in"], 32)
            dve.wait_ge(s["wg_hi"], 1)
            V.scalar_tensor_tensor(wg_s[:, 1, :, :], wg_sb, S_W, wg_s[:, 0, :, :], ALU.mult, ALU.subtract).then_inc(s["wg_lo"], 1)
            head(H - 1, last=True)
            dve.wait_ge(s["gate_done"], 1)
            V.scalar_tensor_tensor(glog, glog_ps, 1.0 / (S_X * S_W), bgbc.unsqueeze(1).to_broadcast([P, T, E]),
                                   ALU.mult, ALU.add).then_inc(s["glog_ready"], 1)
            dve.wait_ge(s["glog_ready"], 1)
            for t in range(T):
                V.max(top8[:, t, :], glog[:, t, :]).then_inc(s["top8_ready"], 1)
            dve.wait_ge(s["top8_ready"], T)
            V.tensor_tensor(gap, top8[:, :, 1], top8[:, :, 0], ALU.subtract).then_inc(s["gap_ready"], 1)
            for t in range(T):
                V.max_index(idx8[:, t, :], top8[:, t, :], glog[:, t, :]).then_inc(s["idx_ready"], 1)
            dve.wait_ge(s["idx_ready"], T)
            V.tensor_copy(idxf, idx8).then_inc(s["idxf_ready"], 1)
            dve.wait_ge(s["route_consts"], 8)
            dve.wait_ge(s["idxf_ready"], 1)
            for k in range(2):
                V.tensor_tensor(one[:, k, :, :], iota_f[:, 0:E].unsqueeze(1).to_broadcast([P, T, E]),
                                idxf[:, :, k:k + 1].to_broadcast([P, T, E]), ALU.is_equal).then_inc(s["onehot_ready"], 1)
            dve.wait_ge(s["onehot_ready"], 2)
            V.tensor_tensor(chosen[:, 0:T, :], one[:, 0, :, :], one[:, 1, :, :], ALU.add).then_inc(s["chosen_ready"], 1)
            dve.wait_ge(s["rank_done"], 1)
            V.tensor_scalar(countsi, rank[:, T, :], float(P - 1), None, ALU.add).then_inc(s["countsi_ready"], 1)
            dve.wait_ge(s["countsi_ready"], 1)
            V.tensor_scalar(padi, countsi, -P, None, ALU.bitwise_and).then_inc(s["padi_ready"], 1)
            dve.wait_ge(s["padi_ready"], 1)
            V.tensor_copy(padf, padi).then_inc(s["padf_ready"], 1)
            dve.wait_ge(s["padf_ready"], 1)
            V.tensor_tensor_scan(ends, onesr, padf, 0.0, ALU.mult, ALU.add).then_inc(s["ends_ready"], 1)
            dve.wait_ge(s["ends_ready"], 1)
            V.tensor_tensor(base, ends, padf, ALU.subtract).then_inc(s["base_e_ready"], 1)
            dve.wait_ge(s["base_e_ready"], 1)
            V.tensor_tensor(slot_e, rank[:, 0:T, :], base.unsqueeze(1).to_broadcast([P, T, E]), ALU.add).then_inc(s["slot_e_ready"], 1)
            dve.wait_ge(s["slot_e_ready"], 1)
            V.tensor_tensor(pick, one, slot_e.unsqueeze(1).to_broadcast([P, 2, T, E]), ALU.mult).then_inc(s["pick_ready"], 1)
            dve.wait_ge(s["pick_ready"], 1)
            V.tensor_reduce(slotf, pick, AX.X, ALU.add).then_inc(s["slotf_ready"], 1)
            dve.wait_ge(s["slotf_ready"], 1)
            V.tensor_copy(sloti, slotf).then_inc(s["sloti_ready"], 1)
            dve.wait_ge(s["sloti_ready"], 1)
            V.tensor_scalar(rowi, sloti, P - 1, None, ALU.bitwise_and).then_inc(s["rowi_ready"], 1)
            dve.wait_ge(s["rowi_ready"], 1)
            V.tensor_copy(rowf, rowi).then_inc(s["rowf_ready"], 1)
            dve.wait_ge(s["rowf_ready"], 1)
            dve.wait_ge(s["yn_stored"], 32)
            V.tensor_tensor(blockf, slotf, rowf, ALU.subtract).then_inc(s["blockf_ready"], 1)
            dve.wait_ge(s["blockf_ready"], 1)
            for k in range(2):
                V.tensor_tensor(block_hot[:, k, :, :], jb_f[:, 0:BLOCKS].unsqueeze(1).to_broadcast([P, T, BLOCKS]),
                                blockf[:, k, :].unsqueeze(2).to_broadcast([P, T, BLOCKS]), ALU.is_equal).then_inc(s["block_hot_ready"], 1)
            for k in range(2):
                for a, b in ((0, TP), (TP, T)):
                    V.tensor_tensor(row_hot[:, k, a:b, :], iota_f.unsqueeze(1).to_broadcast([P, b - a, P]),
                                    rowf[:, k, a:b].unsqueeze(2).to_broadcast([P, b - a, P]), ALU.is_equal).then_inc(s["row_hot_ready"], 1)
            V.tensor_tensor(jcmp[0:1, :, :], jb_f[0:1, :].unsqueeze(2).to_broadcast([1, BLOCKS + 1, E]),
                            ends[0:1, :].unsqueeze(1).to_broadcast([1, BLOCKS + 1, E]), ALU.is_ge).then_inc(s["jcmp_ready"], 1)
            dve.wait_ge(s["token_done"], 1)
            V.scalar_tensor_tensor(spare, token_ps, 0.0, ids[:, T:T + 1].to_broadcast([P, BLOCKS]), ALU.is_equal, ALU.mult
                                   ).then_inc(s["spare_ready"], 1)
            dve.wait_ge(s["spare_ready"], 1)
            V.scalar_tensor_tensor(token, token_ps, -1.0, spare, ALU.add, ALU.add).then_inc(s["token_ready"], 1)
            dve.wait_ge(s["jcmp_ready"], 1)
            V.tensor_reduce(jexp[0:1, :], jcmp[0:1, :, :], AX.X, ALU.add).then_inc(s["jexp_ready"], 1)
            dve.wait_ge(s["jexp_ready"], 1)
            V.tensor_scalar(jexp[0:1, :], jexp[0:1, :], float(E - 1), None, ALU.min).then_inc(s["jmin_ready"], 1)
            dve.wait_ge(s["jmin_ready"], 1)
            word = jexp[0:1, 5:BLOCKS + 1:4]
            for u in range(4, -1, -1):
                dst = block_expert[0:1, :] if u == 0 else jword[0:1, :]
                V.scalar_tensor_tensor(dst, word, float(E), jexp[0:1, u:u + 4 * QUADS - 3:4], ALU.mult, ALU.add
                                       ).then_inc(s["block_expert_ready" if u == 0 else "jmin_ready"], 1)
                if u > 0:
                    dve.wait_ge(s["jmin_ready"], 6 - u)
                word = jword[0:1, :]
            dve.wait_ge(s["expgap_ready"], 1)
            V.tensor_scalar(den, expgap, 1.0, None, ALU.add).then_inc(s["den_ready"], 1)
            dve.wait_ge(s["den_ready"], 1)
            V.reciprocal(gate[:, 0, :], den).then_inc(s["gate1_ready"], 1)
            dve.wait_ge(s["gate1_ready"], 1)
            V.tensor_tensor(gate[:, 1, :], expgap, gate[:, 0, :], ALU.mult).then_inc(s["gate2_ready"], 1)
            dve.wait_ge(s["gate2_ready"], 1)
            V.tensor_tensor(gate, gate, rowok[:, :, 0].unsqueeze(1).to_broadcast([P, 2, T]), ALU.mult).then_inc(s["gate_ready"], 1)
            dve.wait_ge(s["gate_ready"], 1)
            V.tensor_scalar(gate_s[:, 0, :, :], gate, S_G, None, ALU.mult).then_inc(s["gate_hi"], 1)
            dve.wait_ge(s["gate_hi"], 1)
            V.scalar_tensor_tensor(gate_s[:, 1, :, :], gate, S_G, gate_s[:, 0, :, :], ALU.mult, ALU.subtract).then_inc(s["gate_lo"], 1)
            dve.wait_ge(s["gate_lo"], 1)

            def x_parts(j):
                dve.wait_ge(s["ex_T"], j + 1)
                V.tensor_copy(xT.rearrange("p s f n -> p (s f n)"), xt_bank).then_inc(s["ex_x"], 1)

            def w1_low(j, place, e):
                dve.wait_ge(s["experts_ready"], e + 1)
                V.tensor_copy(w1_lo[:, place, :, :].rearrange("p f n -> p (f n)"), w1_s[1][:, bass.ds(e, 1), :, :].rearrange("p e f n -> p (e f n)")
                              ).then_inc(s["ex_w"], 1)

            def h_parts(j):
                for half in range(2):
                    src = hid[:, 512 * half:512 * (half + 1)]
                    hi, lo = (hT[:, k, 4 * half:4 * half + 4, :].rearrange("p f n -> p (f n)") for k in range(2))
                    dve.wait_ge(s["gelu_done"], 2 * j + half + 1)
                    V.tensor_scalar(hi, src, S_H, None, ALU.mult).then_inc(s["ex_h_hi"], 1)
                    dve.wait_ge(s["ex_h_hi"], 2 * j + half + 1)
                    V.scalar_tensor_tensor(lo, src, S_H, hi, ALU.mult, ALU.subtract).then_inc(s["ex_h_lo"], 1)

            def y_rows(j, place, e, ring_used=True):
                if ring_used:
                    dve.wait_ge(s["mixed"], 16 * (j - YR + 1))
                dve.wait_ge(s["ex_o"], j + 1)
                V.scalar_tensor_tensor(yb[:, place, :], ps[:, Y_BANK, 0:D], 1.0 / (S_H * S_W), sl(b2bc, e),
                                       ALU.mult, ALU.add).then_inc(s["y_sum"], 1)
                dve.wait_ge(s["y_sum"], j + 1)
                V.tensor_scalar(yb[:, place, :], yb[:, place, :], col(slot_gate, j), None, ALU.mult).then_inc(s["ys_ready"], 1)

            def quad(i, first=False, last=False):
                e = experts_of(V, i, 6)
                for u in range(4):
                    j = 4 * i + u + 1
                    if not (last and u == 3):
                        x_parts(j + 1)
                        w1_low(j + 1, u % 2, e[u + 2])
                    y_rows(j - 1, u % YR, e[u], not first)
                    h_parts(j)
                if last:
                    y_rows(j, 4 % YR, e[4])

            V.memset(dve_credit[:, 1:2], 0.0).then_inc(s["ex_h_lo"], 2)
            dve.wait_ge(s["b2_loaded"], 16)
            dve.wait_ge(s["block_expert_ready"], 1)
            e = experts_of(V, 0, 2)[1]
            x_parts(0)
            for a in range(2):
                for k in range(2):
                    V.tensor_tensor(block_gate[:, a, k, :, :], block_hot[:, k, :, :],
                                    gate_s[:, a, k, :].unsqueeze(2).to_broadcast([P, T, BLOCKS]), ALU.mult).then_inc(s["block_gate_ready"], 1)
            V.scalar_tensor_tensor(acc[:, :, :], acc[:, :, :], 1.0 / S_ACC, yn, ALU.mult, ALU.add).then_inc(s["base_ready"], 1)
            dve.wait_ge(s["base_ready"], 1)
            x_parts(1)
            w1_low(1, 1, e)
            dve.wait_ge(s["slot_gate_done"], 1)
            V.tensor_scalar(slot_gate, gate_ps, 1.0 / S_G, None, ALU.mult).then_inc(s["slot_gate_ready"], 1)
            dve.wait_ge(s["slot_gate_ready"], 1)
            h_parts(0)
            quad(0, first=True)
            with dve.Fori(1, QUADS - 1) as i:
                quad(i)
            quad(QUADS - 1, last=True)

        @block.tensor
        def _(pe):
            M = nc.tensor

            def three(dst, lhs, rhs, start, stop):
                for n, (a, b) in enumerate(((0, 0), (0, 1), (1, 0))):
                    last = M.matmul(dst, lhs(a), rhs(b), start=start and n == 0, stop=stop and n == 2)
                return last

            def transposed(src, ready, done):
                for k in range(TP + 1):
                    tiles = 2 if k < TP else 1
                    for j in range(tiles):
                        pe.wait_ge(ready, 2 * k + j + 1)
                        for ft in range(DT):
                            last = M.transpose(ps[:, k, (ft * tiles + j) * P:(ft * tiles + j + 1) * P],
                                               src[:, 2 * k + j, ft * P:(ft + 1) * P], ident[:])
                    last.then_inc(done, 1)

            pe.wait_ge(s["consts_ready"], 3)
            transposed(xn, s["xn_ready"], s["xT_done"])
            pe.wait_ge(s["b1_loaded"], 16)
            M.transpose(ps[:, 6, 0:E * FT], b1rows, ident[0:E * FT, 0:E * FT]).then_inc(s["b1_done"], 1)

            def project(h, k, first=False):
                w, dst_dt, half = (wk_s, wq_s, wv_s)[k // 4], k // 2 % 2, k % 2
                t0, _ = head_start(h)
                if first and k % 4 == 0:
                    pe.wait_ge(s["w_lo"], k + 3)
                    pe.wait_ge(s["w_lo_pool"], 1)
                if k >= 4:
                    pe.wait_ge(s["proj_lo"], GROUPS * h + k - 3)
                elif not first and k < 2:
                    pe.wait_ge(s["logits_done"], 3 * T * h)
                elif not first and k == 2:
                    pe.wait_ge(s["p_lo"], 3 * T * h)
                elif not first:
                    pe.wait_ge(s["acc_done"], T * h + 1)
                dst = pair(k)
                for j in range(4):
                    b = 4 * half + j
                    for ft in range(DT):
                        last = three(dst[:, j, 0:WIN], lambda a: w[:, a, ft, b * D + dst_dt * P:b * D + (dst_dt + 1) * P],
                                     lambda c: xnT[:, c, ft, bass.ds(t0, WIN)], ft == 0, ft == DT - 1)
                last.then_inc(s["proj_done"], 1)

            def project_out(h, k):
                if k < 14:
                    pe.wait_ge(s["proj_lo"], GROUPS * h + 12)
                else:
                    pe.wait_ge(s["logits_done"], 3 * T * h + 3)
                dst = pair(k)
                c0, n = PG[k - 12]
                for j in range(n):
                    at = PAD + (c0 + j) * P
                    for ft in range(DT):
                        last = three(dst[:, j, 0:D], lambda a: vT[:, a, ft, at:at + P], lambda c: wo_s[:, c, ft, :],
                                     ft == 0, ft == DT - 1)
                last.then_inc(s["proj_done"], 1)

            def scores(h, t, c, first=False):
                c0, w = CH[c]
                if not first:
                    pe.wait_ge(s["logits_done"], 3 * (h * T + t) + c - 2)
                at = t * P + PAD
                for ft in range(DT):
                    last = three(ps[:, S_BANK[c], 0:w], lambda a: qT[:, a, ft, bass.ds(at, P)] if not first else qT[:, a, ft, PAD:PAD + P],
                                 lambda b: kT[:, b, ft, PAD + c0:PAD + c0 + w], ft == 0, ft == DT - 1)
                last.then_inc(s["qk_done"], 1)

            def transposes(h, t, g_, rows=P):
                i = h * T + t
                if g_ == 0:
                    pe.wait_ge(s["exp_done"], i + 1)
                c0, n = PG[g_]
                for j in range(n):
                    last = M.transpose(ps[:, T_BANK + g_, j * P:j * P + rows], prob[0:rows, (c0 + j) * P:(c0 + j + 1) * P],
                                       ident[0:rows, 0:rows])
                last.then_inc(s["t_done"], 1)

            def attend(h, t):
                i = h * T + t
                pe.wait_ge(s["acc_done"], i + 1)
                for g_, (c0, n) in enumerate(PG):
                    pe.wait_ge(s["p_lo"], 3 * i + g_ + 1)
                    for c in range(c0, c0 + n):
                        k = P if c < T - 1 else TAIL
                        last = three(ps[:, O_BANK, 0:D], lambda a: probT[0:k, a, c * P:(c + 1) * P],
                                     lambda b: vo[0:k, b, c, :], c == 0, c == T - 1)
                last.then_inc(s["av_done"], 1)

            pe.wait_ge(s["xT_lo"], TP + 1)
            pe.wait_ge(s["prob_pad"], 1)
            def head(h, first=False, last=False):
                for k in range(2, 12):
                    project(h, k, first)
                pe.wait_ge(s["proj_lo"], GROUPS * h + 10)
                for c in range(3):
                    scores(h, 0, c, first=True)
                pe.wait_ge(s["wo_free"], h + 2)
                for k in range(12, 15):
                    project_out(h, k)
                with pe.Fori(0, T - 1) as t:
                    scores(h, t + 1, 0)
                    scores(h, t + 1, 1)
                    pe.wait_ge(s["proj_lo"], GROUPS * h + GROUPS)
                    for g_ in range(3):
                        transposes(h, t, g_)
                    scores(h, t + 1, 2)
                    attend(h, t)
                if not last:
                    project(h + 1, 0)
                for g_ in range(3):
                    transposes(h, T - 1, g_, TAIL)
                if not last:
                    project(h + 1, 1)
                attend(h, T - 1)

            project(0, 0, True)
            pe.wait_ge(s["b1_ready"], 1)
            pe.wait_ge(s["pads_ready"], 2)
            project(0, 1, True)
            head(0, first=True)
            with pe.Fori(1, H - 1) as h:
                head(h)
            head(H - 1, last=True)

            pe.wait_ge(s["wg_lo"], 1)
            for t in range(T + 1):
                if t < T:
                    pe.wait_ge(s["ynsp_lo"], t + 1)
                    if t >= 4:
                        pe.wait_ge(s["ynT_ready"], t - 3)
                    for q in range(2 * DT):
                        last = M.transpose(ynT_ps[t % 4][:, q * P:(q + 1) * P], ynsp[:, t, q // DT, (q % DT) * P:(q % DT + 1) * P], ident16[:])
                    last.then_inc(s["ynT_done"], 1)
                if t >= 1:
                    pe.wait_ge(s["ynT_ready"], t)
                    for ft in range(DT):
                        last = three(glog_ps[:, t - 1, :], lambda a: ynT[:, t - 1, a, ft, :], lambda b: wg_s[:, b, ft, :],
                                     ft == 0, ft == DT - 1)
            last.then_inc(s["gate_done"], 1)
            pe.wait_ge(s["route_consts"], 8)
            pe.wait_ge(s["chosen_ready"], 1)
            M.matmul(rank, ones, chosen[:, T:T + 1, :].to_broadcast([P, T + 1, E]), start=True, stop=False)
            for t in range(T):
                k = P if t < T - 1 else TAIL
                M.matmul(rank[:, t + 1:T + 1, :], ones[0:k, :], chosen[0:k, t:t + 1, :].to_broadcast([k, T - t, E]),
                         start=False, stop=False, skip_group_check=True)
            M.matmul(rank, tri, chosen, start=False, stop=True).then_inc(s["rank_done"], 1)
            for k in range(2):
                pe.wait_ge(s["block_id_ready"], k + 1)
                for t in range(T):
                    if t in (0, TP):
                        pe.wait_ge(s["row_hot_ready"], 2 * k + (t > 0) + 1)
                    last = M.matmul(token_ps, row_hot[:, k, t, :], block_id[:, k, t, :], start=k == 0 and t == 0, stop=k == 1 and t == T - 1)
            last.then_inc(s["token_done"], 1)
            def block_T(j, place, first=False):
                pe.wait_ge(s["x_in"], 16 * (j + 1))
                if not first:
                    pe.wait_ge(s["ex_x"], j)
                for q in range(2 * DT):
                    last = M.transpose(xt_bank[:, q * P:(q + 1) * P], xb[:, place, q * P:(q + 1) * P], ident16[:])
                last.then_inc(s["ex_T"], 1)

            def w1_part(e, place, a, k, ft):
                if a == 1 and place is not None:
                    return w1_lo[:, place, k, ft * P:(ft + 1) * P]
                return w1_s[a][:, bass.ds(e, 1), k, ft * P:(ft + 1) * P].rearrange("p e n -> p (e n)")

            def block_H(j, e, place, first=False):
                pe.wait_ge(s["experts_ready"], e + 1)
                pe.wait_ge(s["ex_x"], j + 1)
                if not first:
                    pe.wait_ge(s["ex_w"], j)
                for half in range(2):
                    if not first:
                        pe.wait_ge(s["gelu_done"], 2 * j - 1 + half)
                    for ft in range(4 * half, 4 * half + 4):
                        for k in range(DT):
                            last = three(flat[:, 512 * H_BANK + ft * P:512 * H_BANK + (ft + 1) * P],
                                         lambda a: w1_part(e, place, a, k, ft),
                                         lambda b: xT[:, b, k, :], k == 0, k == DT - 1)
                    last.then_inc(s["ex_h"], 1)

            def block_O(j, e, first=False):
                if not first:
                    pe.wait_ge(s["y_sum"], j)
                for ft in range(FT):
                    if ft % 4 == 0:
                        pe.wait_ge(s["ex_h_lo"], 2 * j + ft // 4 + 3)
                    last = three(ps[:, Y_BANK, 0:D], lambda a: hT[:, a, ft, :],
                                 lambda b: w2_s[b][:, bass.ds(e, 1), ft, :].rearrange("p e n -> p (e n)"), ft == 0, ft == FT - 1)
                last.then_inc(s["ex_o"], 1)

            def quad(i, e, first=False, last=False):
                for u in range(4):
                    j = 4 * i + u + 1
                    block_H(j, e[u + 1], (u + 1) % 2)
                    if not (last and u == 3):
                        block_T(j + 1, (u + 2) % XR)
                    block_O(j - 1, e[u], first and u == 0)
                if last:
                    block_O(j, e[4])

            pe.wait_ge(s["block_expert_ready"], 1)
            e = experts_of(M, 0)
            block_T(0, 0, first=True)
            block_H(0, e[0], None, first=True)
            block_T(1, 1)
            pe.wait_ge(s["block_gate_ready"], 4)
            for k in range(2):
                for t in range(T):
                    for a in range(2):
                        last = M.matmul(gate_ps, row_hot[:, k, t, :], block_gate[:, a, k, t, :],
                                        start=k == 0 and t == 0 and a == 0, stop=k == 1 and t == T - 1 and a == 1)
            last.then_inc(s["slot_gate_done"], 1)
            quad(0, e, first=True)
            with pe.Fori(1, QUADS - 1) as i:
                quad(i, experts_of(M, i))
            quad(QUADS - 1, experts_of(M, QUADS - 1), last=True)


_INS = ["x", "adj", "L0_gnn_Wq", "L0_gnn_Wk", "L0_gnn_Wv", "L0_gnn_Wout", "L0_ffn_Wg", "L0_ffn_bg",
        "L0_ffn_W1", "L0_ffn_b1", "L0_ffn_W2", "L0_ffn_b2"]


def kernel(**inputs):
    import numpy as _np
    import concourse.bacc as _bacc
    from concourse import mybir as _mybir
    from concourse.bass_utils import run_bass_kernel_spmd as _run

    nc = _bacc.Bacc("TRN2", target_bir_lowering=False, num_devices=1)
    arrays, args = {}, []
    for name in _INS:
        a = _np.ascontiguousarray(inputs[name])
        arrays[f"in_{name}_dram"] = a
        args.append(nc.dram_tensor(f"in_{name}_dram", a.shape, _mybir.dt.from_np(a.dtype), kind="ExternalInput").ap())
    args.append(nc.dram_tensor("out_0_dram", (N + P, D), F32, kind="ExternalOutput").ap())
    args.append(nc.dram_tensor("w_split_dram", (E * P, 4, 2048), F16, kind="Internal").ap())
    args.append(nc.dram_tensor("yn_rows_dram", (N + P, 2 * D), F16, kind="Internal").ap())
    build(nc, *args)
    r = _run(nc, [arrays], core_ids=[0])
    return r.results[0]["out_0_dram"][0:N]
```
